# Optimizing a Trainium2 kernel written in Bass

```python
import numpy as np
import jax
import jax.numpy as jnp

def _softmax(x, axis=-1):
    return jax.nn.softmax(x, axis=axis)

def _gelu(x):
    return jax.nn.gelu(x, approximate=True)

def _silu(x):
    return jax.nn.silu(x)

def _sigmoid(x):
    return jax.nn.sigmoid(x)

def _layernorm(x, axis=-1, eps=1e-05):
    m = jnp.mean(x, axis=axis, keepdims=True)
    v = jnp.var(x, axis=axis, keepdims=True)
    return (x - m) / jnp.sqrt(v + eps)

def _scatter_add(tgt, idx, src, axis=0):
    return tgt.at[idx].add(src)

def _segment_sum(src, seg, n):
    return jax.ops.segment_sum(src, seg, n)
kernel_name = 'mk_recurrent_d2_jaxref_r8_2af2d1'

def setup_inputs(seed: int=0):
    np.random.seed(seed)
    _w = jnp.asarray

    def _L0_attn_setup():
        import jax, jax.numpy as jnp
        import numpy as np
        HEADS = 16

        def _binarize(W):
            alpha = jnp.mean(jnp.abs(W), axis=tuple(range(1, W.ndim)), keepdims=True)
            B = W + jax.lax.stop_gradient(jnp.sign(W) - W)
            return alpha * B

        def _binlinear(x, W, b):
            Wb = _binarize(W)
            return jnp.einsum('btc,oc->bto', x, Wb) + b
        key = jax.random.key(seed)
        ks = jax.random.split(key, 9)
        dim = 128
        B, T = (4, 256)
        inp = {'x': jax.random.normal(ks[0], (B, T, dim), jnp.float32), 'Wq': jax.random.normal(ks[1], (dim, dim), jnp.float32) * 0.02, 'bq': jax.random.normal(ks[2], (dim,), jnp.float32) * 0.02, 'Wk': jax.random.normal(ks[3], (dim, dim), jnp.float32) * 0.02, 'bk': jax.random.normal(ks[4], (dim,), jnp.float32) * 0.02, 'Wv': jax.random.normal(ks[5], (dim, dim), jnp.float32) * 0.02, 'bv': jax.random.normal(ks[6], (dim,), jnp.float32) * 0.02, 'Wp': jax.random.normal(ks[7], (dim, dim), jnp.float32) * 0.02, 'bp': jax.random.normal(ks[8], (dim,), jnp.float32) * 0.02}
        return inp
    _L0_attn_in = _L0_attn_setup()

    def _L0_ffn_setup():
        import jax, jax.numpy as jnp
        import numpy as np
        B, S, H = (4, 256, 128)
        D = 256
        E = 8
        K = 2
        key = jax.random.key(seed)
        ks = jax.random.split(key, 8)
        w = lambda k, shape: jax.random.normal(k, shape, jnp.float32) * 0.02
        return {'hidden_states': jax.random.normal(ks[0], (B, S, H), jnp.float32), 'gate_w': w(ks[1], (H, E)), 'w_gate': w(ks[2], (E, H, D)), 'w_up': w(ks[3], (E, H, D)), 'w_down': w(ks[4], (E, D, H)), 'ws_gate': w(ks[5], (H, D)), 'ws_up': w(ks[6], (H, D)), 'ws_down': w(ks[7], (D, H))}
    _L0_ffn_in = _L0_ffn_setup()

    def _L1_attn_setup():
        import jax, jax.numpy as jnp
        import numpy as np
        import math
        B, L, D_MODEL = (2, 256, 128)
        NUM_HEADS = 16
        FEATURE_DIM = 16
        HEAD_DIM = D_MODEL // NUM_HEADS
        EPS = 1e-12

        def taylor_exp(x):
            d = x.shape[-1]
            r2 = math.sqrt(2.0)
            rd = math.sqrt(d)
            rrd = math.sqrt(rd)
            x2 = (x[..., :, None] * x[..., None, :]).reshape(*x.shape[:-1], d * d) / r2
            ones = jnp.ones_like(x[..., :1])
            return jnp.concatenate([ones, x / rrd, x2 / rd], axis=-1)
        key = jax.random.key(seed)
        k0, k1, k2, k3, k4 = jax.random.split(key, 5)
        hidden_states = jax.random.normal(k0, (B, L, D_MODEL), dtype=jnp.float32)
        s = 1.0 / math.sqrt(D_MODEL)
        Wq = jax.random.normal(k1, (FEATURE_DIM * NUM_HEADS, D_MODEL), dtype=jnp.float32) * s
        Wk = jax.random.normal(k2, (FEATURE_DIM * NUM_HEADS, D_MODEL), dtype=jnp.float32) * s
        Wv = jax.random.normal(k3, (NUM_HEADS * HEAD_DIM, D_MODEL), dtype=jnp.float32) * s
        Wo = jax.random.normal(k4, (D_MODEL, NUM_HEADS * HEAD_DIM), dtype=jnp.float32) * s
        return {'hidden_states': hidden_states, 'Wq': Wq, 'Wk': Wk, 'Wv': Wv, 'Wo': Wo}
    _L1_attn_in = _L1_attn_setup()

    def _L1_ffn_setup():
        import jax, jax.numpy as jnp
        import numpy as np
        B, S, DIM = (4, 512, 128)
        BASE_COUPLING = 0.1
        NUM_CYCLES = 3

        def _gelu(x):
            return jax.nn.gelu(x, approximate=False)

        def _coupling_net(h, w1, b1, w2, b2, w3, b3, w4, b4):
            h = _gelu(h @ w1 + b1)
            h = _gelu(h @ w2 + b2)
            h = _gelu(h @ w3 + b3)
            return jax.nn.sigmoid(h @ w4 + b4)

        def _global_net(h, w1, b1, w2, b2, w3, b3):
            h = _gelu(h @ w1 + b1)
            h = _gelu(h @ w2 + b2)
            return jax.nn.sigmoid(h @ w3 + b3)

        def _twist(x):
            o_r, o_i, p_r, p_i = jnp.split(x, 4, axis=-1)
            return jnp.concatenate([p_r, -p_i, -o_r, o_i], axis=-1)
        key = jax.random.key(seed)
        ks = jax.random.split(key, 9)
        d = DIM

        def w(k, fan_in, fan_out):
            return jax.random.normal(k, (fan_in, fan_out), dtype=jnp.float32) / np.sqrt(fan_in).astype(np.float32)
        inp = {'x': jax.random.normal(ks[0], (B, S, d), dtype=jnp.float32)}
        cn_dims = [(d, d), (d, d // 2), (d // 2, d // 4), (d // 4, 1)]
        for i, (a, b) in enumerate(cn_dims):
            inp[f'cn_w{i + 1}'] = w(ks[1 + i], a, b)
            inp[f'cn_b{i + 1}'] = jnp.zeros((b,), dtype=jnp.float32)
        gc_dims = [(d, d // 2), (d // 2, d // 4), (d // 4, 1)]
        for i, (a, b) in enumerate(gc_dims):
            inp[f'gc_w{i + 1}'] = w(ks[5 + i], a, b)
            inp[f'gc_b{i + 1}'] = jnp.zeros((b,), dtype=jnp.float32)
        inp['adaptive_range'] = jnp.full((1,), 0.2, dtype=jnp.float32)
        return inp
    _L1_ffn_in = _L1_ffn_setup()
    _d = {'L0_attn_x': _L0_attn_in['x'], 'L0_attn_Wq': _L0_attn_in['Wq'], 'L0_attn_bq': _L0_attn_in['bq'], 'L0_attn_Wk': _L0_attn_in['Wk'], 'L0_attn_bk': _L0_attn_in['bk'], 'L0_attn_Wv': _L0_attn_in['Wv'], 'L0_attn_bv': _L0_attn_in['bv'], 'L0_attn_Wp': _L0_attn_in['Wp'], 'L0_attn_bp': _L0_attn_in['bp'], 'L0_ffn_gate_w': _L0_ffn_in['gate_w'], 'L0_ffn_w_gate': _L0_ffn_in['w_gate'], 'L0_ffn_w_up': _L0_ffn_in['w_up'], 'L0_ffn_w_down': _L0_ffn_in['w_down'], 'L0_ffn_ws_gate': _L0_ffn_in['ws_gate'], 'L0_ffn_ws_up': _L0_ffn_in['ws_up'], 'L0_ffn_ws_down': _L0_ffn_in['ws_down'], 'L1_attn_Wq': _L1_attn_in['Wq'], 'L1_attn_Wk': _L1_attn_in['Wk'], 'L1_attn_Wv': _L1_attn_in['Wv'], 'L1_attn_Wo': _L1_attn_in['Wo'], 'L1_ffn_cn_w1': _L1_ffn_in['cn_w1'], 'L1_ffn_cn_b1': _L1_ffn_in['cn_b1'], 'L1_ffn_cn_w2': _L1_ffn_in['cn_w2'], 'L1_ffn_cn_b2': _L1_ffn_in['cn_b2'], 'L1_ffn_cn_w3': _L1_ffn_in['cn_w3'], 'L1_ffn_cn_b3': _L1_ffn_in['cn_b3'], 'L1_ffn_cn_w4': _L1_ffn_in['cn_w4'], 'L1_ffn_cn_b4': _L1_ffn_in['cn_b4'], 'L1_ffn_gc_w1': _L1_ffn_in['gc_w1'], 'L1_ffn_gc_b1': _L1_ffn_in['gc_b1'], 'L1_ffn_gc_w2': _L1_ffn_in['gc_w2'], 'L1_ffn_gc_b2': _L1_ffn_in['gc_b2'], 'L1_ffn_gc_w3': _L1_ffn_in['gc_w3'], 'L1_ffn_gc_b3': _L1_ffn_in['gc_b3'], 'L1_ffn_adaptive_range': _L1_ffn_in['adaptive_range']}
    _x0 = _d['L0_attn_x']
    _d['L0_attn_x'] = jax.random.normal(jax.random.fold_in(jax.random.key(seed), 1), (8, 512, 128), dtype=_x0.dtype)
    del _x0
    return _d

def reference(L0_attn_x, L0_attn_Wq, L0_attn_bq, L0_attn_Wk, L0_attn_bk, L0_attn_Wv, L0_attn_bv, L0_attn_Wp, L0_attn_bp, L0_ffn_gate_w, L0_ffn_w_gate, L0_ffn_w_up, L0_ffn_w_down, L0_ffn_ws_gate, L0_ffn_ws_up, L0_ffn_ws_down, L1_attn_Wq, L1_attn_Wk, L1_attn_Wv, L1_attn_Wo, L1_ffn_cn_w1, L1_ffn_cn_b1, L1_ffn_cn_w2, L1_ffn_cn_b2, L1_ffn_cn_w3, L1_ffn_cn_b3, L1_ffn_cn_w4, L1_ffn_cn_b4, L1_ffn_gc_w1, L1_ffn_gc_b1, L1_ffn_gc_w2, L1_ffn_gc_b2, L1_ffn_gc_w3, L1_ffn_gc_b3, L1_ffn_adaptive_range):

    def _L0_attn_ref(x, Wq, bq, Wk, bk, Wv, bv, Wp, bp):
        import jax, jax.numpy as jnp
        import numpy as np
        HEADS = 16

        def _binarize(W):
            alpha = jnp.mean(jnp.abs(W), axis=tuple(range(1, W.ndim)), keepdims=True)
            B = W + jax.lax.stop_gradient(jnp.sign(W) - W)
            return alpha * B

        def _binlinear(x, W, b):
            Wb = _binarize(W)
            return jnp.einsum('btc,oc->bto', x, Wb) + b
        B, T, C = x.shape
        H = HEADS
        Dh = C // H
        scale = Dh ** (-0.5)

        def split_heads(t):
            return t.reshape(B, T, H, Dh).transpose(0, 2, 1, 3)
        q = split_heads(_binlinear(x, Wq, bq))
        k = split_heads(_binlinear(x, Wk, bk))
        v = split_heads(_binlinear(x, Wv, bv))
        att = jnp.einsum('bhtd,bhsd->bhts', q, k) * scale
        att = jax.nn.softmax(att, axis=-1)
        y = jnp.einsum('bhts,bhsd->bhtd', att, v)
        y = y.transpose(0, 2, 1, 3).reshape(B, T, C)
        return _binlinear(y, Wp, bp)

    def _L0_ffn_ref(hidden_states, gate_w, w_gate, w_up, w_down, ws_gate, ws_up, ws_down):
        import jax, jax.numpy as jnp
        import numpy as np
        B, S, H = (4, 256, 128)
        D = 256
        E = 8
        K = 2
        b, s, h = hidden_states.shape
        x = hidden_states.reshape(-1, h)
        scores = jax.nn.softmax(x @ gate_w, axis=-1)
        topk_w, topk_idx = jax.lax.top_k(scores, K)
        topk_w = topk_w / (jnp.sum(topk_w, axis=-1, keepdims=True) + 1e-20)
        onehot = jax.nn.one_hot(topk_idx, E, dtype=x.dtype)
        w_per_expert = jnp.einsum('nke,nk->ne', onehot, topk_w)
        y = jnp.zeros_like(x)
        for e in range(E):
            hid = jax.nn.silu(x @ w_gate[e]) * (x @ w_up[e])
            y = y + w_per_expert[:, e:e + 1] * (hid @ w_down[e])
        shared = jax.nn.silu(x @ ws_gate) * (x @ ws_up) @ ws_down
        return (y + shared).reshape(b, s, h)

    def _L1_attn_ref(hidden_states, Wq, Wk, Wv, Wo):
        import jax, jax.numpy as jnp
        import numpy as np
        import math
        B, L, D_MODEL = (2, 256, 128)
        NUM_HEADS = 16
        FEATURE_DIM = 16
        HEAD_DIM = D_MODEL // NUM_HEADS
        EPS = 1e-12

        def taylor_exp(x):
            d = x.shape[-1]
            r2 = math.sqrt(2.0)
            rd = math.sqrt(d)
            rrd = math.sqrt(rd)
            x2 = (x[..., :, None] * x[..., None, :]).reshape(*x.shape[:-1], d * d) / r2
            ones = jnp.ones_like(x[..., :1])
            return jnp.concatenate([ones, x / rrd, x2 / rd], axis=-1)
        b, l, _ = hidden_states.shape
        q = (hidden_states @ Wq.T).reshape(b, l, NUM_HEADS, FEATURE_DIM).transpose(0, 2, 1, 3)
        k = (hidden_states @ Wk.T).reshape(b, l, NUM_HEADS, FEATURE_DIM).transpose(0, 2, 1, 3)
        v = (hidden_states @ Wv.T).reshape(b, l, NUM_HEADS, HEAD_DIM).transpose(0, 2, 1, 3)
        qf = taylor_exp(q)
        kf = taylor_exp(k)
        A = jnp.einsum('bhnd,bhmd->bhnm', qf, kf)
        A = jnp.tril(A)
        y = jnp.einsum('bhnm,bhme->bhne', A, v)
        z = 1.0 / (jnp.einsum('bhld,bhld->bhl', qf, jnp.cumsum(kf, axis=2)) + EPS)
        y = y * z[..., None]
        y = y.transpose(0, 2, 1, 3).reshape(b, l, NUM_HEADS * HEAD_DIM)
        return y @ Wo.T

    def _L1_ffn_ref(x, cn_w1, cn_b1, cn_w2, cn_b2, cn_w3, cn_b3, cn_w4, cn_b4, gc_w1, gc_b1, gc_w2, gc_b2, gc_w3, gc_b3, adaptive_range):
        import jax, jax.numpy as jnp
        import numpy as np
        B, S, DIM = (4, 512, 128)
        BASE_COUPLING = 0.1
        NUM_CYCLES = 3

        def _gelu(x):
            return jax.nn.gelu(x, approximate=False)

        def _coupling_net(h, w1, b1, w2, b2, w3, b3, w4, b4):
            h = _gelu(h @ w1 + b1)
            h = _gelu(h @ w2 + b2)
            h = _gelu(h @ w3 + b3)
            return jax.nn.sigmoid(h @ w4 + b4)

        def _global_net(h, w1, b1, w2, b2, w3, b3):
            h = _gelu(h @ w1 + b1)
            h = _gelu(h @ w2 + b2)
            return jax.nn.sigmoid(h @ w3 + b3)

        def _twist(x):
            o_r, o_i, p_r, p_i = jnp.split(x, 4, axis=-1)
            return jnp.concatenate([p_r, -p_i, -o_r, o_i], axis=-1)
        global_context = x.mean(axis=1, keepdims=True)
        gf = _global_net(global_context, gc_w1, gc_b1, gc_w2, gc_b2, gc_w3, gc_b3)
        out = x
        for _ in range(NUM_CYCLES):
            tf = _coupling_net(out, cn_w1, cn_b1, cn_w2, cn_b2, cn_w3, cn_b3, cn_w4, cn_b4)
            combined = 0.7 * gf + 0.3 * tf
            coupling = BASE_COUPLING + adaptive_range * (combined - 0.5) * 2.0
            out = out + coupling * _twist(out)
        return out
    x = L0_attn_x
    xn = _layernorm(x, axis=-1)
    s = _L0_attn_ref(xn, L0_attn_Wq, L0_attn_bq, L0_attn_Wk, L0_attn_bk, L0_attn_Wv, L0_attn_bv, L0_attn_Wp, L0_attn_bp)
    g = _silu(_L0_ffn_ref(xn, L0_ffn_gate_w, L0_ffn_w_gate, L0_ffn_w_up, L0_ffn_w_down, L0_ffn_ws_gate, L0_ffn_ws_up, L0_ffn_ws_down))
    x = x + s * g
    xn = _layernorm(x, axis=-1)
    s = _L1_attn_ref(xn, L1_attn_Wq, L1_attn_Wk, L1_attn_Wv, L1_attn_Wo)
    g = _silu(_L1_ffn_ref(xn, L1_ffn_cn_w1, L1_ffn_cn_b1, L1_ffn_cn_w2, L1_ffn_cn_b2, L1_ffn_cn_w3, L1_ffn_cn_b3, L1_ffn_cn_w4, L1_ffn_cn_b4, L1_ffn_gc_w1, L1_ffn_gc_b1, L1_ffn_gc_w2, L1_ffn_gc_b2, L1_ffn_gc_w3, L1_ffn_gc_b3, L1_ffn_adaptive_range))
    x = x + s * g
    return x

_drawn_inputs = setup_inputs


def setup_inputs(seed=0):
    import zlib

    import numpy as np

    out = dict(_drawn_inputs(seed))
    spreads = {'L1_ffn_cn_b1': (0.0, 2.0),
     'L1_ffn_cn_b2': (0.0, 2.0),
     'L1_ffn_cn_b3': (0.0, 2.0),
     'L1_ffn_gc_b1': (0.0, 2.0),
     'L1_ffn_gc_b2': (0.0, 2.0)}
    factors = {'L0_attn_Wq': 8.0,
     'L0_attn_bq': 8.0,
     'L0_attn_Wk': 8.0,
     'L0_attn_bk': 200.0,
     'L0_attn_Wv': 8.0,
     'L0_attn_bv': 8.0,
     'L0_attn_Wp': 8.0,
     'L0_attn_bp': 8.0,
     'L0_ffn_gate_w': 8.0,
     'L0_ffn_w_gate': 8.0,
     'L0_ffn_w_up': 8.0,
     'L0_ffn_w_down': 8.0,
     'L0_ffn_ws_gate': 8.0,
     'L0_ffn_ws_up': 8.0,
     'L0_ffn_ws_down': 8.0,
     'L1_ffn_cn_w1': 200.0,
     'L1_ffn_cn_w2': 200.0,
     'L1_ffn_cn_w3': 200.0,
     'L1_ffn_cn_w4': 200.0,
     'L1_ffn_gc_w1': 8.0,
     'L1_ffn_gc_w2': 8.0,
     'L1_ffn_gc_w3': 8.0,
     'L1_attn_Wq': 3.086,
     'L1_attn_Wk': 3.023}
    for name, (base, spread) in spreads.items():
        noise = np.random.default_rng([zlib.crc32(name.encode()), seed]).standard_normal(out[name].shape)
        drawn = base * np.exp(spread * noise) if base else spread * noise
        out[name] = jnp.asarray(drawn.astype(out[name].dtype))
    for name, factor in factors.items():
        out[name] = (out[name] * factor).astype(out[name].dtype)
    return out
```

```python
from contextlib import ExitStack

import numpy as np

import concourse.bass as bass
from concourse import mybir

F32 = mybir.dt.float32
BF16 = mybir.dt.bfloat16
U32 = mybir.dt.uint32
ALU = mybir.AluOpType
ACT = mybir.ActivationFunctionType
AX_X = mybir.AxisListType.X

P = 128
C = 128
B, T = 8, 512
TT = T // P
NT = B * TT
H, DH = 16, 8
DQ1 = 16
GH = 4
NG = H // GH
STRIP = P // GH
NCOMP = C + H
STEPS = NG * TT
PAIRS = ((0, 0), (0, 1), (1, 0), (1, 1), (0, 2), (2, 0))
KROWS = 96
EPS_LN = 1e-5
EXPERTS, DFF = 8, 256
CHUNKS = DFF // P
EPS_L1 = 1e-12


def wait(engine, semaphore, count):
    if isinstance(count, int) and count <= 0:
        return
    engine.wait_ge(semaphore, count)


def shape_constants():
    ident = np.eye(P, dtype=np.float32)
    tri = np.triu(np.ones((P, P), np.float32))
    ones = np.ones((P, P), np.float32)
    sel = np.zeros((P, NG, NCOMP), np.float32)
    for g in range(NG):
        for j in range(GH):
            for d in range(DH):
                sel[STRIP * j + d, g, (GH * g + j) * DH + d] = 1.0
            sel[STRIP * j + DH, g, C + GH * g + j] = 1.0
    q = C // 4
    twist = np.zeros((P, P), np.float32)
    for i in range(q):
        twist[2 * q + i, i] = 1.0
        twist[3 * q + i, q + i] = -1.0
        twist[i, 2 * q + i] = -1.0
        twist[q + i, 3 * q + i] = 1.0
    lower = np.zeros((P, EXPERTS * EXPERTS), np.float32)
    lower[:] = np.tril(np.ones((EXPERTS, EXPERTS), np.float32), -1).ravel()
    return np.concatenate([ident, tri, ones, sel.reshape(P, -1), twist, lower], axis=1)


CONST_COLS = 3 * P + NG * NCOMP + P + EXPERTS * EXPERTS


def build_program(nc, io):
    with ExitStack() as whole:
        def keep(name, shape, dt=F32):
            return whole.enter_context(nc.sbuf_tensor(name, shape, dt))

        S = {}
        S["bank"] = [whole.enter_context(nc.psum_tensor(f"bank{i}", [P, T], F32)) for i in range(2)]
        S["quad"] = whole.enter_context(nc.psum_tensor("quad", [P, 4, T], F32))
        S["av"] = whole.enter_context(nc.psum_tensor("av", [P, T], F32))
        S["misc"] = whole.enter_context(nc.psum_tensor("misc", [P, T], F32))
        S["const"] = keep("const", [P, CONST_COLS])
        o = 0
        for name, n in (("ident", P), ("tri", P), ("ones", P), ("sel", NG * NCOMP), ("twist", P), ("lower", EXPERTS * EXPERTS)):
            S[name] = S["const"][:, o:o + n]
            o += n
        S["x"] = keep("x_tok", [P, NT, C])
        S["xnT"] = keep("xnT", [C, B * T])
        S["s"] = keep("s_tok", [P, NT, C])
        S["wT"] = keep("wT", [C, 4 * C])
        S["bqk"] = keep("bqk", [C, 2])
        S["bv"] = keep("bv", [P, C])
        S["bp"] = keep("bp", [P, C])
        S["w1T"] = keep("w1T", [C, 6 * C])
        for name, a, b in (("wq1T", 0, 2), ("wk1T", 2, 4), ("wv1T", 4, 5), ("wo1T", 5, 6)):
            S[name] = S["w1T"][:, a * C:b * C]
        S["route"] = keep("route", [P, NT, EXPERTS])
        prepare_weights(nc, io, S)
        layer_norm(nc, io, S, "ln0", io["L0_attn_x"])
        attention0(nc, io, S)
        route(nc, io, S)
        moe(nc, io, S)
        layer_norm(nc, io, S, "ln1", None)
        coupling(nc, io, S)
        attention1(nc, io, S)


def prepare_weights(nc, io, S):
    names = ("Wq", "Wk", "Wv", "Wp")
    with ExitStack() as ctx:
        def sb(name, shape, dt=F32):
            return ctx.enter_context(nc.sbuf_tensor(name, shape, dt))

        def sem(name):
            return ctx.enter_context(nc.semaphore(name))

        w = sb("w_raw", [P, 4, C])
        w1 = sb("w1_raw", [P, 6, C])
        sign = sb("w_sign", [P, 4, C])
        diff = sb("w_diff", [P, 4, C])
        binary = sb("w_bin", [P, 4, C])
        scaled = sb("w_scaled", [P, 4, C])
        alpha = sb("w_alpha", [P, 8])
        loaded = sem("w_loaded")
        loaded1 = sem("w1_loaded")
        small = sem("w_small_loaded")
        signed = sem("w_signed")
        summed = sem("w_summed")
        meaned = sem("w_meaned")
        differed = sem("w_differed")
        rebuilt = sem("w_rebuilt")
        multiplied = sem("w_multiplied")
        turned = sem("w_turned")
        copied = sem("w_copied")
        block = ctx.enter_context(nc.Block())

        @block.sync
        def _(sp):
            sp.dma_start(S["const"][:, :], io["shape_constants"]).then_inc(loaded, 16)
            for n, name in enumerate(names):
                if n >= 2:
                    sp.dma_start(w[:, n, :], io["L0_attn_" + name]).then_inc(loaded, 32)
                    continue
                for f in range(2):
                    rows = slice(64 * f, 64 * (f + 1))
                    sp.dma_start(w[rows, n, :], io["L0_attn_" + name][rows, :].rearrange("(h d) c -> d h c", d=DH))\
                      .then_inc(loaded, 16)
                    sp.dma_start(S["bqk"][rows, n:n + 1],
                                 io["L0_attn_bq" if n == 0 else "L0_attn_bk"][rows].rearrange("(h d o) -> d h o", d=DH, o=1),
                                 allow_slow_non_contiguous=True)\
                      .then_inc(small, 16)
            sp.dma_start(S["bv"][:, :], io["L0_attn_bv"].rearrange("(o c) -> o c", o=1).broadcast_to([P, C])).then_inc(small, 16)
            sp.dma_start(S["bp"][:, :], io["L0_attn_bp"].rearrange("(o c) -> o c", o=1).broadcast_to([P, C])).then_inc(small, 16)
            for n, name in enumerate(("Wq", "Wk")):
                for k in range(2):
                    src = io["L1_attn_" + name][k * P:(k + 1) * P, :].rearrange("(h d) c -> d h c", d=DQ1)
                    sp.dma_start(w1[:, 2 * n + k, :], src).then_inc(loaded1, 16)
            for n, name in enumerate(("Wv", "Wo")):
                sp.dma_start(w1[:, 4 + n, :], io["L1_attn_" + name]).then_inc(loaded1, 16)
            sp.wait_ge(small, 96)

        @block.scalar
        def _(act):
            act.wait_ge(loaded, 16 * 9)
            act.activation(sign[:, :, :], w[:, :, :], ACT.Sign).then_inc(signed, 1)
            act.wait_ge(turned, 1)
            act.activation(S["w1T"][:, 0:T], S["quad"][:, 0, :], ACT.Copy)
            act.activation(S["w1T"][:, T:], S["quad"][:, 1, 0:2 * P], ACT.Copy)
            act.wait_ge(turned, 2)
            act.activation(S["wT"][:, :], S["misc"][:, :], ACT.Copy).then_inc(copied, 1)

        @block.vector
        def _(dve):
            dve.wait_ge(loaded, 16 * 9)
            dve.tensor_reduce(alpha[:, 0:4], w[:, :, :], AX_X, ALU.add, apply_absolute_value=True).then_inc(summed, 1)
            dve.wait_ge(signed, 1)
            dve.tensor_tensor(diff[:, :, :], sign[:, :, :], w[:, :, :], ALU.subtract).then_inc(differed, 1)
            dve.wait_ge(summed, 1)
            dve.tensor_scalar(alpha[:, 4:8], alpha[:, 0:4], 1.0 / C, None, ALU.mult).then_inc(meaned, 1)
            dve.wait_ge(differed, 1)
            dve.tensor_tensor(binary[:, :, :], w[:, :, :], diff[:, :, :], ALU.add).then_inc(rebuilt, 1)
            dve.wait_ge(rebuilt, 1)
            dve.wait_ge(meaned, 1)
            dve.tensor_tensor(scaled[:, :, :], binary[:, :, :], alpha[:, 4:8, None].broadcast_to([P, 4, C]), ALU.mult).then_inc(multiplied, 1)

        @block.tensor
        def _(pe):
            pe.wait_ge(loaded, 16 * 9)
            pe.wait_ge(loaded1, 16 * 6)
            for n in range(6):
                last = pe.transpose(S["quad"][:, n // 4, (n % 4) * P:(n % 4 + 1) * P], w1[:, n, :], S["ident"])
            last.then_inc(turned, 1)
            pe.wait_ge(multiplied, 1)
            for n in range(4):
                last = pe.transpose(S["misc"][:, n * P:(n + 1) * P], scaled[:, n, :], S["ident"])
            last.then_inc(turned, 1)


def layer_norm(nc, io, S, tag, source):
    x, xnT = S["x"], S["xnT"]
    with ExitStack() as ctx:
        def sb(name, shape, dt=F32):
            return ctx.enter_context(nc.sbuf_tensor(f"{tag}_{name}", shape, dt))

        def sem(name):
            return ctx.enter_context(nc.semaphore(f"{tag}_{name}"))

        xc = sb("centred", [P, NT, C])
        sq = sb("squares", [P, 2, TT, C])
        total = sb("total", [P, NT])
        mean = sb("mean", [P, NT])
        var = sb("var", [P, NT])
        vare = sb("vare", [P, NT])
        std = sb("std", [P, NT])
        rstd = sb("rstd", [P, NT])
        loaded = [sem(f"loaded{c}") for c in range(B)]
        totalled = sem("totalled")
        meaned = sem("meaned")
        centred = sem("centred_done")
        squared = sem("squared")
        spread = sem("spread")
        shifted = sem("shifted")
        rooted = sem("rooted")
        inverted = sem("inverted")
        scaled = sem("scaled")
        turned = sem("turned")
        stored = sem("stored")
        block = ctx.enter_context(nc.Block())

        def tiles(c):
            return slice(TT * c, TT * (c + 1))

        if source is not None:
            @block.sync
            def _(sp):
                xv = source.rearrange("b (t p) c -> b p t c", p=P)
                for c in range(B):
                    sp.dma_start(x[:, tiles(c), :], xv[c]).then_inc(loaded[c], 16)

        @block.vector
        def _(dve):
            for c in range(B):
                if source is not None:
                    dve.wait_ge(loaded[c], 16)
                dve.tensor_reduce(total[:, tiles(c)], x[:, tiles(c), :], AX_X, ALU.add).then_inc(totalled, 1)
                dve.wait_ge(totalled, c + 1)
                dve.tensor_scalar(mean[:, tiles(c)], total[:, tiles(c)], 1.0 / C, None, ALU.mult).then_inc(meaned, 1)
                if c >= 1:
                    dve.wait_ge(squared, c)
                    dve.tensor_reduce(var[:, tiles(c - 1)], sq[:, (c - 1) % 2], AX_X, ALU.add).then_inc(spread, 1)
                dve.wait_ge(meaned, c + 1)
                dve.tensor_tensor(xc[:, tiles(c), :], x[:, tiles(c), :], mean[:, tiles(c), None].broadcast_to([P, TT, C]),
                                  ALU.subtract).then_inc(centred, 1)
            dve.wait_ge(squared, B)
            dve.tensor_reduce(var[:, tiles(B - 1)], sq[:, (B - 1) % 2], AX_X, ALU.add).then_inc(spread, 1)
            dve.wait_ge(spread, B)
            dve.tensor_scalar(vare[:, :], var[:, :], 1.0 / C, EPS_LN, ALU.mult, ALU.add).then_inc(shifted, 1)
            dve.wait_ge(rooted, 1)
            dve.reciprocal(rstd[:, :], std[:, :]).then_inc(inverted, 1)
            dve.wait_ge(inverted, 1)
            for c in range(B):
                dve.tensor_tensor(xc[:, tiles(c), :], xc[:, tiles(c), :], rstd[:, tiles(c), None].broadcast_to([P, TT, C]),
                                  ALU.mult).then_inc(scaled, 1)

        @block.scalar
        def _(act):
            for c in range(B):
                act.wait_ge(centred, c + 1)
                if c >= 2:
                    act.wait_ge(spread, c - 1)
                act.activation(sq[:, c % 2], xc[:, tiles(c), :], ACT.Square).then_inc(squared, 1)
            act.wait_ge(shifted, 1)
            act.activation(std[:, :], vare[:, :], ACT.Sqrt).then_inc(rooted, 1)
            for c in range(B):
                act.wait_ge(turned, c + 1)
                act.activation(xnT[:, T * c:T * (c + 1)], S["bank"][c % 2][:, :], ACT.Copy).then_inc(stored, 1)

        @block.tensor
        def _(pe):
            for c in range(B):
                pe.wait_ge(scaled, c + 1)
                if c >= 2:
                    pe.wait_ge(stored, c - 1)
                for t in range(TT):
                    last = pe.transpose(S["bank"][c % 2][:, t * P:(t + 1) * P], xc[:, TT * c + t, :], S["ident"])
                last.then_inc(turned, 1)


def attention0(nc, io, S):
    scale = DH ** -0.5
    with ExitStack() as ctx:
        def sb(name, shape, dt=F32):
            return ctx.enter_context(nc.sbuf_tensor("a0_" + name, shape, dt))

        def sem(name):
            return ctx.enter_context(nc.semaphore("a0_" + name))

        xs = [sb(f"xs{i}", [C, T]) for i in range(2)]
        full = [sb(f"full{i}", [P, T]) for i in range(2)]
        rest = [sb(f"rest{i}", [P, T]) for i in range(2)]
        parts = [sb(f"parts{i}", [P, 3, T], BF16) for i in range(2)]
        qs = [sb(f"qs{i}", [P, H, T], BF16) for i in range(2)]
        ks = [sb(f"ks{i}", [P, H, T], BF16) for i in range(2)]
        va = [sb(f"va{i}", [P, TT, H, STRIP]) for i in range(2)]
        probs = sb("probs", [P, 8, T])
        osb = [sb(f"osb{i}", [P, NG, T]) for i in range(2)]
        nmax = [sb(f"nmax{i}", [P, P]) for i in range(2)]
        nrest = sb("nrest", [STRIP, P])
        nparts = sb("nparts", [STRIP, 3, P], BF16)
        rden = sb("rden", [P, 2, H])
        yn = sb("yn", [P, TT, C])
        yT = sb("yT", [C, T])
        so = sb("so", [P, TT, C])

        cleared = sem("cleared")
        onesset = sem("ones_set")
        xs_in = sem("xs_in")
        q_mm, k_mm, v_mm = sem("q_mm"), sem("k_mm"), sem("v_mm")
        qk_read = sem("qk_read")
        rested = sem("rested")
        second = sem("second")
        split = sem("split")
        stack_a, stack_b = sem("stack_a"), sem("stack_b")
        v_read = sem("v_read")
        max_mm, max_red = sem("max_mm"), sem("max_red")
        nm_mm = sem("nm_mm")
        n0, n1, n2 = sem("n0"), sem("n1"), sem("n2")
        ns_done = sem("ns_done")
        mrows = sem("mrows")
        s_mm, exped = sem("s_mm"), sem("exped")
        av_mm, o_read = sem("av_mm"), sem("o_read")
        c_mm, rec, yn_done = sem("c_mm"), sem("rec"), sem("yn_done")
        yt_mm, yt_read = sem("yt_mm"), sem("yt_read")
        pr_mm, so_done, so_out = sem("pr_mm"), sem("so_done"), sem("so_out")
        bank, quad, av, misc = S["bank"], S["quad"], S["av"], S["misc"]
        wT = S["wT"]
        block = ctx.enter_context(nc.Block())

        STACK = 16 * 2 * len(PAIRS)


        @block.sync
        def _(sp):
            def known(value):
                return value if isinstance(value, int) else sp.snap(sp.to_reg(value))

            def load_xs(b, par, col):
                col = known(col)
                mine, used = known(16 * b), known(b - 1)
                wait(sp, xs_in, mine)
                wait(sp, v_mm, used)
                sp.dma_start(xs[par][:, :], S["xnT"][:, bass.ds(col, T)]).then_inc(xs_in, 16)

            def stack(b, par, half):
                done = stack_b if half else stack_a
                split_now, scores_now, before = known(2 * b + 2), known(64 * (b - 2) + 32 * (half + 1)), known(STACK * b)
                wait(sp, done, before)
                wait(sp, split, split_now)
                wait(sp, s_mm, scores_now)
                rows = slice(64 * half, 64 * half + 64)
                heads = slice(8 * half, 8 * half + 8)
                for n, (i, j) in enumerate(PAIRS):
                    for op, (dst, part) in enumerate(((qs, i), (ks, j))):
                        src = parts[op][rows, part, :]
                        sp.dma_start(dst[par][DH * n:DH * (n + 1), heads, :], src).then_inc(done, 16)

            def max_rows(b, par, half):
                split_now, before = known(2 * b + half + 1), known(48 * (2 * b + half))
                wait(sp, mrows, before)
                wait(sp, ns_done, split_now)
                for i in range(3):
                    sp.dma_start(qs[par][KROWS + i:KROWS + i + 1, 8 * half:8 * half + 8, :],
                                 nparts[:, i, :]).then_inc(mrows, 16)

            def store_s(b, tile0):
                tile0, summed, before = known(tile0), known(b + 1), known(16 * b)
                wait(sp, so_out, before)
                wait(sp, so_done, summed)
                sp.dma_start(S["s"][:, bass.ds(tile0, TT), :], so[:, :, :]).then_inc(so_out, 16)

            def main(i, par, n):
                if n <= 5:
                    load_xs(i + 2, par, (i + 2) * T)
                max_rows(i, par, 1)
                if n >= 1:
                    store_s(i - 1, (i - 1) * TT)
                if n <= 5:
                    stack(i + 2, par, 0)
                if n <= 6:
                    max_rows(i + 1, 1 - par, 0)
                if n <= 5:
                    stack(i + 2, par, 1)

            sp.wait_ge(cleared, 3)
            sp.wait_ge(onesset, 1)
            load_xs(0, 0, 0)
            load_xs(1, 1, T)
            for b in range(2):
                stack(b, b, 0)
                stack(b, b, 1)
            max_rows(0, 0, 0)
            main(0, 0, 0)
            main(1, 1, 1)
            with sp.Fori(1, 3) as j:
                main(j * 2, 0, 2)
                main(j * 2 + 1, 1, 3)
            main(6, 0, 6)
            main(7, 1, 7)
            store_s(7, 7 * TT)
            sp.wait_ge(so_out, 16 * B)

        @block.gpsimd
        def _(pool):
            pool.memset(qs[0][:, :, :].bitcast(U32), 0).then_inc(cleared, 1)
            pool.memset(ks[0][:, :, :].bitcast(U32), 0).then_inc(cleared, 1)
            pool.memset(qs[1][:, :, :].bitcast(U32), 0).then_inc(cleared, 1)

            def split_one(b, op):
                f, r, pt = full[op], rest[op], parts[op]
                wait(pool, qk_read, 2 * b + op + 1)
                pool.tensor_tensor(r[:, :], f[:, :], pt[:, 0, :], ALU.subtract).then_inc(rested, 1)
                pool.tensor_tensor(pt[:, 1, :], f[:, :], pt[:, 0, :], ALU.subtract).then_inc(second, 1)
                wait(pool, rested, 2 * b + op + 1)
                wait(pool, second, 2 * b + op + 1)
                pool.tensor_tensor(pt[:, 2, :], r[:, :], pt[:, 1, :], ALU.subtract).then_inc(split, 1)

            for b in range(2):
                for op in range(2):
                    split_one(b, op)
            for i in range(2):
                for op in range(2):
                    split_one(i + 2, op)
            with pool.Fori(1, 3) as j:
                for n in range(2):
                    for op in range(2):
                        split_one(j * 2 + n + 2, op)

        @block.tensor
        def _(pe):
            def q_k(b, par, op):
                if op == 0:
                    wait(pe, xs_in, 16 * (b + 1))
                pe.matmul(misc[:, :], wT[:, op * C:(op + 1) * C], xs[par][:, :], start=True, stop=True)\
                  .then_inc(k_mm if op else q_mm, 1)

            def values(b, par):
                for t in range(TT):
                    last = pe.matmul(misc[:, t * P:(t + 1) * P], xs[par][:, t * P:(t + 1) * P], wT[:, 2 * C:3 * C],
                                     start=True, stop=True)
                last.then_inc(v_mm, 1)

            def max_tile(b, par, u):
                h, qt = u // TT, u % TT
                if u == 0:
                    wait(pe, stack_a, STACK * (b + 1))
                if u == 32:
                    wait(pe, stack_b, STACK * (b + 1))
                if u % 2 == 0:
                    wait(pe, max_red, 32 * b + u // 2 - 1)
                mm = pe.matmul(quad[:, 2 * ((u // 2) % 2) + u % 2, :], qs[par][0:KROWS, h, qt * P:(qt + 1) * P],
                               ks[par][0:KROWS, h, :], start=True, stop=True)
                if u % 2:
                    mm.then_inc(max_mm, 1)

            def max_turn(b, half):
                wait(pe, max_red, 32 * b + 16 * (half + 1))
                pe.transpose(misc[:, 0:P], nmax[half][:, :], S["ident"]).then_inc(nm_mm, 1)

            def score(b, par, t, j):
                g, kt = t // TT, t % TT
                h, n = GH * g + j, 4 * t + j
                if t == 0 and j == 0:
                    wait(pe, mrows, 96 * b + 48)
                if t == 8 and j == 0:
                    wait(pe, mrows, 96 * b + 96)
                wait(pe, exped, 64 * b + n - 1)
                pe.matmul(bank[n % 2][:, :], ks[par][0:KROWS + 3, h, kt * P:(kt + 1) * P], qs[par][0:KROWS + 3, h, :],
                          start=True, stop=True).then_inc(s_mm, 1)

            def weigh(b, par, t):
                g, kt = t // TT, t % TT
                wait(pe, exped, 64 * b + 4 * t + 4)
                if kt == 0:
                    wait(pe, o_read, 4 * b + g)
                if t == 0:
                    wait(pe, v_read, b + 1)
                for j in range(GH):
                    last = pe.matmul(av[STRIP * j:STRIP * (j + 1), :], va[par][:, kt, GH * g + j, :],
                                     probs[:, (4 * t + j) % 8, :], start=(kt == 0), stop=(kt == TT - 1))
                last.then_inc(av_mm, 1)

            def gather(b, par, pair):
                if pair == 0:
                    wait(pe, o_read, 4 * b + 4)
                for k in range(2):
                    t = 2 * pair + k
                    for g in range(NG):
                        last = pe.matmul(misc[:, k * NCOMP:(k + 1) * NCOMP], osb[par][:, g, t * P:(t + 1) * P],
                                         S["sel"][:, g * NCOMP:(g + 1) * NCOMP], start=(g == 0), stop=(g == NG - 1))
                last.then_inc(c_mm, 1)

            def turn_y(b):
                wait(pe, yn_done, 2 * b + 2)
                for t in range(TT):
                    last = pe.transpose(misc[:, t * P:(t + 1) * P], yn[:, t, :], S["ident"])
                last.then_inc(yt_mm, 1)

            def project(b):
                wait(pe, yt_read, b + 1)
                for t in range(TT):
                    last = pe.matmul(misc[:, t * P:(t + 1) * P], yT[:, t * P:(t + 1) * P], wT[:, 3 * C:4 * C],
                                     start=True, stop=True)
                last.then_inc(pr_mm, 1)

            def finish_step(i, par, k, n):
                if k == 0:
                    gather(i, par, 0)
                elif k == 1:
                    wait(pe, yn_done, 2 * i + 1)
                    gather(i, par, 1)
                elif k == 2:
                    turn_y(i)
                else:
                    project(i)

            def main(i, par, n):
                for t in range(STEPS):
                    for j in range(GH):
                        score(i, par, t, j)
                        if n <= 6:
                            max_tile(i + 1, 1 - par, 4 * t + j)
                    if t >= 1:
                        weigh(i, par, t - 1)
                    elif n >= 1:
                        weigh(i - 1, 1 - par, STEPS - 1)
                    if t == 1:
                        wait(pe, so_done, i - 1)
                        wait(pe, ns_done, 2 * i + 1)
                        max_turn(i, 1)
                    if t == 2 and n <= 5:
                        wait(pe, ns_done, 2 * i + 2)
                        q_k(i + 2, par, 0)
                    if t == 3 and n <= 5:
                        wait(pe, qk_read, 2 * i + 5)
                        q_k(i + 2, par, 1)
                    if t == 4 and n <= 6:
                        wait(pe, qk_read, 2 * i + 6) if n <= 5 else wait(pe, ns_done, 2 * i + 2)
                        values(i + 1, 1 - par)
                    if 5 <= t <= 8 and n >= 1:
                        if t == 5:
                            wait(pe, v_read, i + 2) if n <= 6 else wait(pe, ns_done, 2 * i + 2)
                        finish_step(i - 1, 1 - par, t - 5, n)
                    if t == 9 and n <= 6:
                        wait(pe, so_done, i) if n >= 1 else wait(pe, v_read, i + 2)
                        max_turn(i + 1, 0)

            q_k(0, 0, 0)
            pe.wait_ge(qk_read, 1)
            q_k(0, 0, 1)
            pe.wait_ge(qk_read, 2)
            q_k(1, 1, 0)
            pe.wait_ge(qk_read, 3)
            q_k(1, 1, 1)
            pe.wait_ge(qk_read, 4)
            values(0, 0)
            for u in range(4 * STEPS):
                max_tile(0, 0, u)
            pe.wait_ge(v_read, 1)
            max_turn(0, 0)
            main(0, 0, 0)
            main(1, 1, 1)
            with pe.Fori(1, 3) as j:
                main(j * 2, 0, 2)
                main(j * 2 + 1, 1, 3)
            main(6, 0, 6)
            main(7, 1, 7)
            weigh(7, 1, STEPS - 1)
            pe.wait_ge(so_done, 7)
            for k in range(4):
                finish_step(7, 1, k, 8)

        @block.scalar
        def _(act):
            def read_qk(b, op):
                wait(act, k_mm if op else q_mm, b + 1)
                wait(act, stack_b, STACK * b)
                wait(act, split, 2 * b - 1 + op)
                act.activation(full[op][:, :], misc[:, :], ACT.Identity, bias=S["bqk"][:, op:op + 1])
                act.activation(parts[op][:, 0, :], misc[:, :], ACT.Identity, bias=S["bqk"][:, op:op + 1])\
                   .then_inc(qk_read, 1)

            def exps(b, t):
                for j in range(GH):
                    n = 4 * t + j
                    if j == 0:
                        wait(act, av_mm, 16 * b + t - 1)
                    wait(act, s_mm, 64 * b + n + 1)
                    act.activation(probs[:, n % 8, :], bank[n % 2][:, :], ACT.Exp, scale=scale).then_inc(exped, 1)

            def read_o(b, par, g):
                wait(act, av_mm, 16 * b + 4 * g + 4)
                wait(act, c_mm, 2 * (b - 1))
                act.activation(osb[par][:, g, :], av[:, :], ACT.Copy).then_inc(o_read, 1)

            def read_yT(b):
                wait(act, yt_mm, b + 1)
                wait(act, pr_mm, b)
                act.activation(yT[:, :], misc[:, :], ACT.Copy).then_inc(yt_read, 1)

            def main(i, par, n):
                for t in range(STEPS):
                    exps(i, t)
                    if t == 0 and n >= 1:
                        read_o(i - 1, 1 - par, NG - 1)
                    if t > 0 and t % TT == 0:
                        read_o(i, par, t // TT - 1)
                    if t == 2 and n <= 5:
                        read_qk(i + 2, 0)
                    if t == 3 and n <= 5:
                        read_qk(i + 2, 1)
                    if t == 7 and n >= 1:
                        read_yT(i - 1)

            for b in range(2):
                for op in range(2):
                    read_qk(b, op)
            main(0, 0, 0)
            main(1, 1, 1)
            with act.Fori(1, 3) as j:
                main(j * 2, 0, 2)
                main(j * 2 + 1, 1, 3)
            main(6, 0, 6)
            main(7, 1, 7)
            read_o(7, 1, NG - 1)
            read_yT(7)

        @block.vector
        def _(dve):
            dve.memset(ks[1][:, :, :].bitcast(U32), 0).then_inc(n0, 1)
            for i in range(2):
                dve.memset(va[i][:, :, :, :].bitcast(U32), 0).then_inc(n0, 1)
                dve.memset(nmax[i][:, :], 0.0)
            dve.wait_ge(n0, 3)
            dve.wait_ge(cleared, 3)
            for i in range(2):
                dve.memset(ks[i][KROWS:KROWS + 3, :, :], 1.0)
                last = dve.memset(va[i][:, :, :, DH:DH + 1], 1.0)
            last.then_inc(onesset, 1)

            def read_v(b, par):
                wait(dve, v_mm, b + 1)
                wait(dve, av_mm, 16 * (b - 1))
                dve.tensor_tensor(va[par][:, :, :, 0:DH], misc[:, :].rearrange("p (t h d) -> p t h d", t=TT, d=DH),
                                  S["bv"][:, None, :].broadcast_to([P, TT, C]).rearrange("p t (h d) -> p t h d", d=DH),
                                  ALU.add).then_inc(v_read, 1)

            def maxima(b, w):
                half = w // 16
                if w % 16 == 0:
                    wait(dve, nm_mm, 2 * b - 1 + half)
                wait(dve, max_mm, 32 * b + w + 1)
                dve.tensor_reduce(nmax[half][:, 2 * (w % 16):2 * (w % 16) + 2], quad[:, 2 * (w % 2):2 * (w % 2) + 2, :],
                                  AX_X, ALU.max, negate=True).then_inc(max_red, 1)

            def split_max(b, half):
                c = 2 * b + half + 1
                wait(dve, nm_mm, c)
                wait(dve, mrows, 48 * (c - 1))
                m = misc[0:STRIP, 0:P]
                dve.tensor_copy(nparts[:, 0, :], m).then_inc(n1, 1)
                wait(dve, n1, c)
                dve.tensor_tensor(nrest[:, :], m, nparts[:, 0, :], ALU.subtract)
                dve.tensor_tensor(nparts[:, 1, :], m, nparts[:, 0, :], ALU.subtract).then_inc(n2, 1)
                wait(dve, n2, c)
                dve.tensor_tensor(nparts[:, 2, :], nrest[:, :], nparts[:, 1, :], ALU.subtract).then_inc(ns_done, 1)

            def divide(b, pair):
                c = 2 * b + pair + 1
                wait(dve, c_mm, c)
                m = misc[:, 0:2 * NCOMP].rearrange("p (k n) -> p k n", k=2)
                dve.reciprocal(rden[:, :, :], m[:, :, C:NCOMP]).then_inc(rec, 1)
                wait(dve, rec, c)
                if pair == 0:
                    wait(dve, yt_mm, b)
                dve.tensor_tensor(yn[:, 2 * pair:2 * pair + 2, :].rearrange("p k (h d) -> p k h d", d=DH),
                                  m[:, :, 0:C].rearrange("p k (h d) -> p k h d", d=DH),
                                  rden[:, :, :, None].broadcast_to([P, 2, H, DH]), ALU.mult).then_inc(yn_done, 1)

            def read_s(b):
                wait(dve, pr_mm, b + 1)
                wait(dve, so_out, 16 * b)
                dve.tensor_tensor(so[:, :, :], misc[:, :].rearrange("p (t c) -> p t c", t=TT),
                                  S["bp"][:, None, :].broadcast_to([P, TT, C]), ALU.add).then_inc(so_done, 1)

            def main(i, par, n):
                for t in range(STEPS):
                    if n <= 6:
                        maxima(i + 1, 2 * t)
                        maxima(i + 1, 2 * t + 1)
                    if t == 1:
                        split_max(i, 1)
                    if t == 4 and n <= 6:
                        read_v(i + 1, 1 - par)
                    if t in (5, 6) and n >= 1:
                        divide(i - 1, t - 5)
                    if t == 8 and n >= 1:
                        read_s(i - 1)
                    if t == 9 and n <= 6:
                        split_max(i + 1, 0)

            read_v(0, 0)
            for w in range(2 * STEPS):
                maxima(0, w)
            split_max(0, 0)
            main(0, 0, 0)
            main(1, 1, 1)
            with dve.Fori(1, 3) as j:
                main(j * 2, 0, 2)
                main(j * 2 + 1, 1, 3)
            main(6, 0, 6)
            main(7, 1, 7)
            divide(7, 0)
            divide(7, 1)
            read_s(7)


def route(nc, io, S):
    E = EXPERTS
    with ExitStack() as ctx:
        def sb(name, shape, dt=F32):
            return ctx.enter_context(nc.sbuf_tensor("r_" + name, shape, dt))

        def sem(name):
            return ctx.enter_context(nc.semaphore("r_" + name))

        gate = sb("gate", [C, E])
        top = sb("top", [P, NT])
        shifted = sb("shifted", [P, NT, E])
        expo = sb("expo", [P, NT, E])
        total = sb("total", [P, NT])
        inv = sb("inv", [P, NT])
        prob = sb("prob", [P, NT, E])
        above = sb("above", [P, NT, E, E])
        level = sb("level", [P, NT, E, E])
        rank = sb("rank", [P, NT, E])
        chosen = sb("chosen", [P, NT, E])
        norm = sb("norm", [P, NT])
        loaded = sem("loaded")
        scored = sem("scored")
        step = sem("vector_step")
        exponents = sem("exponents")
        block = ctx.enter_context(nc.Block())
        logits = S["misc"][:, 0:NT * E].rearrange("p (t e) -> p t e", e=E)

        @block.sync
        def _(sp):
            sp.dma_start(gate[:, :], io["L0_ffn_gate_w"]).then_inc(loaded, 16)

        @block.tensor
        def _(pe):
            pe.wait_ge(loaded, 16)
            for t in range(NT):
                last = pe.matmul(S["misc"][:, E * t:E * (t + 1)], S["xnT"][:, P * t:P * (t + 1)], gate[:, :],
                                 start=True, stop=True)
            last.then_inc(scored, 1)

        @block.scalar
        def _(act):
            act.wait_ge(step, 2)
            act.activation(expo[:, :, :], shifted[:, :, :], ACT.Exp).then_inc(exponents, 1)

        @block.vector
        def _(dve):
            def over(a):
                return a[:, :, None].broadcast_to([P, NT, E])

            dve.wait_ge(scored, 1)
            dve.tensor_reduce(top[:, :], logits, AX_X, ALU.max).then_inc(step, 1)
            dve.wait_ge(step, 1)
            dve.tensor_tensor(shifted[:, :, :], logits, over(top), ALU.subtract).then_inc(step, 1)
            dve.wait_ge(exponents, 1)
            dve.tensor_reduce(total[:, :], expo[:, :, :], AX_X, ALU.add).then_inc(step, 1)
            dve.wait_ge(step, 3)
            dve.reciprocal(inv[:, :], total[:, :]).then_inc(step, 1)
            dve.wait_ge(step, 4)
            dve.tensor_tensor(prob[:, :, :], expo[:, :, :], over(inv), ALU.mult).then_inc(step, 1)
            dve.wait_ge(step, 5)
            other = prob[:, :, None, :].broadcast_to([P, NT, E, E])
            own = prob[:, :, :, None].broadcast_to([P, NT, E, E])
            dve.tensor_tensor(above[:, :, :, :], other, own, ALU.is_gt)
            dve.tensor_tensor(level[:, :, :, :], other, own, ALU.is_ge).then_inc(step, 1)
            dve.wait_ge(step, 6)
            lower = S["lower"].rearrange("p (o e j) -> p o e j", o=1, e=E).broadcast_to([P, NT, E, E])
            dve.tensor_tensor(level[:, :, :, :], level[:, :, :, :], lower, ALU.mult).then_inc(step, 1)
            dve.wait_ge(step, 7)
            dve.tensor_tensor(level[:, :, :, :], level[:, :, :, :], above[:, :, :, :], ALU.max).then_inc(step, 1)
            dve.wait_ge(step, 8)
            dve.tensor_reduce(rank[:, :, :], level[:, :, :, :], AX_X, ALU.add).then_inc(step, 1)
            dve.wait_ge(step, 9)
            dve.scalar_tensor_tensor(out=chosen[:, :, :], in0=rank[:, :, :], scalar=1.5, in1=prob[:, :, :],
                                     op0=ALU.is_lt, op1=ALU.mult).then_inc(step, 1)
            dve.wait_ge(step, 10)
            dve.tensor_reduce(norm[:, :], chosen[:, :, :], AX_X, ALU.add).then_inc(step, 1)
            dve.wait_ge(step, 11)
            dve.tensor_scalar(top[:, :], norm[:, :], 1e-20, None, ALU.add).then_inc(step, 1)
            dve.wait_ge(step, 12)
            dve.reciprocal(inv[:, :], top[:, :]).then_inc(step, 1)
            dve.wait_ge(step, 13)
            dve.tensor_tensor(S["route"][:, :, :], chosen[:, :, :], over(inv), ALU.mult).then_inc(step, 1)


def moe(nc, io, S):
    E = EXPERTS
    UNITS = CHUNKS * (E + 1)
    with ExitStack() as ctx:
        def sb(name, shape, dt=F32):
            return ctx.enter_context(nc.sbuf_tensor("m_" + name, shape, dt))

        def sem(name):
            return ctx.enter_context(nc.semaphore("m_" + name))

        wg = sb("wg", [C, E + 1, DFF])
        wu = sb("wu", [C, E + 1, DFF])
        wd = sb("wd", [P, E + 1, CHUNKS, C])
        xs = [sb(f"xs{i}", [C, T]) for i in range(2)]
        xt = [sb(f"xt{i}", [P, TT, C]) for i in range(2)]
        st = [sb(f"st{i}", [P, TT, C]) for i in range(2)]
        wt = [sb(f"wt{i}", [P, TT, E]) for i in range(2)]
        xw = [sb(f"xw{i}", [C, T]) for i in range(2)]
        act_g = [sb(f"act{i}", [P, T]) for i in range(2)]
        hid = [sb(f"hid{i}", [P, T]) for i in range(2)]
        gated = sb("gated", [P, TT, C])
        prod = sb("prod", [P, TT, C])
        xo = [sb(f"xo{i}", [P, TT, C]) for i in range(2)]
        weights_in = [sem(f"weights_in{i}") for i in range(2)]
        inputs_in = sem("inputs_in")
        wb_mm, xw_done = sem("wb_mm"), sem("xw_done")
        g_mm, u_mm, d_mm = sem("g_mm"), sem("u_mm"), sem("d_mm")
        silu_done, h_done = sem("silu_done"), sem("h_done")
        out_mm, out_silu, prod_done, x_done, x_out = (sem("out_mm"), sem("out_silu"), sem("prod_done"), sem("x_done"),
                                                      sem("x_out"))
        gate_bank, up_bank = S["bank"], S["quad"]
        wb_bank = S["misc"]

        def out_bank(par):
            return S["quad"][:, 2 + par, :]

        block = ctx.enter_context(nc.Block())

        @block.sync
        def _(sp):
            def known(value):
                return value if isinstance(value, int) else sp.snap(sp.to_reg(value))

            sp.dma_start(wg[:, 0, :], io["L0_ffn_ws_gate"]).then_inc(weights_in[0], 16)
            sp.dma_start(wu[:, 0, :], io["L0_ffn_ws_up"]).then_inc(weights_in[0], 16)
            sp.dma_start(wd[:, 0, :, :], io["L0_ffn_ws_down"].rearrange("(k p) o -> p k o", p=P)).then_inc(weights_in[0], 16)

            def load(b, par):
                tile0, col = known(b * TT), known(b * T)
                before, scaled, finished, used = known(64 * b), known(8 * (b - 1)), known(b - 1), known(UNITS * (b - 1))
                wait(sp, inputs_in, before)
                wait(sp, xw_done, scaled)
                wait(sp, u_mm, used)
                wait(sp, x_done, finished)
                sp.dma_start(xs[par][:, :], S["xnT"][:, bass.ds(col, T)]).then_inc(inputs_in, 16)
                sp.dma_start(wt[par][:, :, :], S["route"][:, bass.ds(tile0, TT), :]).then_inc(inputs_in, 16)
                sp.dma_start(xt[par][:, :, :], S["x"][:, bass.ds(tile0, TT), :]).then_inc(inputs_in, 16)
                sp.dma_start(st[par][:, :, :], S["s"][:, bass.ds(tile0, TT), :]).then_inc(inputs_in, 16)

            def store(b, par):
                tile0, before, done = known(b * TT), known(16 * b), known(b + 1)
                wait(sp, x_out, before)
                wait(sp, x_done, done)
                sp.dma_start(S["x"][:, bass.ds(tile0, TT), :], xo[par][:, :, :]).then_inc(x_out, 16)

            load(0, 0)
            sp.dma_start(wg[:, 1:, :], io["L0_ffn_w_gate"].rearrange("e c d -> c e d")).then_inc(weights_in[1], 16)
            sp.dma_start(wu[:, 1:, :], io["L0_ffn_w_up"].rearrange("e c d -> c e d")).then_inc(weights_in[1], 16)
            for k in range(CHUNKS):
                sp.dma_start(wd[:, 1:, k, :], io["L0_ffn_w_down"][:, k * P:(k + 1) * P, :].rearrange("e p o -> p e o"))\
                  .then_inc(weights_in[1], 16)
            load(1, 1)
            with sp.Fori(0, B // 2 - 1) as j:
                for par in range(2):
                    store(j * 2 + par, par)
                    load(j * 2 + par + 2, par)
            store(B - 2, 0)
            store(B - 1, 1)
            sp.wait_ge(x_out, 16 * B)

        @block.tensor
        def _(pe):
            def spread(b, par, e):
                wait(pe, xw_done, 8 * b + e)
                for t in range(TT):
                    last = pe.matmul(wb_bank[:, t * P:(t + 1) * P], wt[par][:, t, e:e + 1].broadcast_to([P, P]), S["ident"],
                                     start=True, stop=True)
                last.then_inc(wb_mm, 1)

            def gate_up(b, par, u):
                e, k = u // CHUNKS, u % CHUNKS
                cols = slice(k * P, (k + 1) * P)
                wait(pe, silu_done, UNITS * b + u - 1)
                pe.matmul(gate_bank[u % 2][:, :], wg[:, e, cols], xs[par][:, :], start=True, stop=True).then_inc(g_mm, 1)
                wait(pe, h_done, UNITS * b + u - 1)
                if e and k == 0:
                    wait(pe, xw_done, 8 * b + e)
                moving = xw[(e - 1) % 2] if e else xs[par]
                pe.matmul(up_bank[:, u % 2, :], wu[:, e, cols], moving[:, :], start=True, stop=True).then_inc(u_mm, 1)

            def down(b, par, u):
                e, k = u // CHUNKS, u % CHUNKS
                wait(pe, h_done, UNITS * b + u + 1)
                if u == 0:
                    wait(pe, out_silu, b - 1)
                for t in range(TT):
                    last = pe.matmul(out_bank(par)[:, t * P:(t + 1) * P], hid[u % 2][:, t * P:(t + 1) * P], wd[:, e, k, :],
                                     start=(u == 0 and t == 0), stop=(u == UNITS - 1), skip_group_check=True)
                last.then_inc(d_mm, 1)

            def sequence(b, par, first=False):
                wait(pe, inputs_in, 64 * (b + 1))
                for u in range(UNITS):
                    if u % CHUNKS == 0 and u // CHUNKS < E:
                        spread(b, par, u // CHUNKS)
                    if first and u == CHUNKS:
                        pe.wait_ge(weights_in[1], 64)
                    gate_up(b, par, u)
                    if u >= 1:
                        down(b, par, u - 1)
                down(b, par, UNITS - 1)

            pe.wait_ge(weights_in[0], 48)
            sequence(0, 0, True)
            sequence(1, 1)
            with pe.Fori(1, B // 2) as j:
                for par in range(2):
                    sequence(j * 2 + par, par)

        @block.scalar
        def _(act):
            def sequence(b, par):
                for u in range(UNITS):
                    wait(act, g_mm, UNITS * b + u + 1)
                    wait(act, h_done, UNITS * b + u - 1)
                    act.activation(act_g[u % 2][:, :], gate_bank[u % 2][:, :], ACT.Silu).then_inc(silu_done, 1)
                wait(act, d_mm, UNITS * (b + 1))
                wait(act, prod_done, b)
                act.activation(gated[:, :, :], out_bank(par).rearrange("p (t c) -> p t c", t=TT), ACT.Silu).then_inc(out_silu, 1)

            sequence(0, 0)
            sequence(1, 1)
            with act.Fori(1, B // 2) as j:
                for par in range(2):
                    sequence(j * 2 + par, par)

        @block.vector
        def _(dve):
            def weigh(b, par, e):
                wait(dve, wb_mm, 8 * b + e + 1)
                wait(dve, u_mm, UNITS * b + 2 * e if e >= 2 else UNITS * b - 2 + 2 * e - 0)
                dve.tensor_tensor(xw[e % 2][:, :], wb_bank[:, :], xs[par][:, :], ALU.mult).then_inc(xw_done, 1)

            def finish(b, par):
                wait(dve, out_silu, b + 1)
                dve.tensor_tensor(prod[:, :, :], gated[:, :, :], st[par][:, :, :], ALU.mult).then_inc(prod_done, 1)
                wait(dve, prod_done, b + 1)
                wait(dve, x_out, 16 * (b - 1))
                dve.tensor_tensor(xo[par][:, :, :], prod[:, :, :], xt[par][:, :, :], ALU.add).then_inc(x_done, 1)

            def sequence(b, par):
                wait(dve, inputs_in, 64 * (b + 1))
                for u in range(UNITS):
                    if u % CHUNKS == 0 and u // CHUNKS < E:
                        weigh(b, par, u // CHUNKS)
                    wait(dve, silu_done, UNITS * b + u + 1)
                    wait(dve, u_mm, UNITS * b + u + 1)
                    wait(dve, d_mm, UNITS * b + u - 1)
                    dve.tensor_tensor(hid[u % 2][:, :], act_g[u % 2][:, :], up_bank[:, u % 2, :], ALU.mult).then_inc(h_done, 1)
                finish(b, par)

            sequence(0, 0)
            sequence(1, 1)
            with dve.Fori(1, B // 2) as j:
                for par in range(2):
                    sequence(j * 2 + par, par)


def coupling(nc, io, S):
    CYCLES = 3
    D2, D3 = C // 2, C // 4
    with ExitStack() as ctx:
        def sb(name, shape, dt=F32):
            return ctx.enter_context(nc.sbuf_tensor("c_" + name, shape, dt))

        def sem(name):
            return ctx.enter_context(nc.semaphore("c_" + name))

        out = sb("out", [C, B * T])
        w1, w2, w3, w4 = sb("w1", [C, C]), sb("w2", [C, D2]), sb("w3", [P, D3]), sb("w4", [P, 1])
        v1, v2, v3 = sb("v1", [C, D2]), sb("v2", [P, D3]), sb("v3", [P, 1])
        bias = sb("bias", [P, 8])
        half = sb("half", [P, 4])
        h1 = [sb(f"h1_{i}", [P, T]) for i in range(2)]
        h2, h3 = sb("h2", [P, T]), sb("h3", [P, T])
        tf = sb("tf", [P, T])
        coup = sb("coup", [P, T])
        delta = sb("delta", [P, T])
        means = sb("means", [C, B])
        context = sb("context", [C, B])
        g1, g2, gt, base = sb("g1", [P, B]), sb("g2", [P, B]), sb("gt", [P, B]), sb("base", [P, B])
        gate = [sb(f"gate{i}", [C, T]) for i in range(2)]
        loaded, copied, zeroed = sem("loaded"), sem("copied"), sem("zeroed")
        prepared = sem("prepared")
        g_mm, g_act, g_vec = sem("g_mm"), sem("g_act"), sem("g_vec")
        mm = [sem(f"mm{i}") for i in range(4)]
        lay = [sem(f"layer{i}") for i in range(4)]
        twisted = sem("twisted")
        coupled, delta_done, updated = sem("coupled"), sem("delta_done"), sem("updated")
        gated, turned, stored = sem("gated"), sem("turned"), sem("stored")
        bank, quad, misc = S["bank"], S["quad"], S["misc"]
        block = ctx.enter_context(nc.Block())
        B1, B2, B3, B4, G1, G2, G3, AR = range(8)

        def cols(t):
            return slice(T * t, T * (t + 1))

        @block.sync
        def _(sp):
            n = 0
            for dst, name, rows in ((w1, "cn_w1", C), (w2, "cn_w2", C), (w3, "cn_w3", D2), (w4, "cn_w4", D3),
                                    (v1, "gc_w1", C), (v2, "gc_w2", D2), (v3, "gc_w3", D3)):
                if rows < C:
                    sp.wait_ge(zeroed, 1)
                sp.dma_start(dst[0:rows, :], io["L1_ffn_" + name]).then_inc(loaded, 16)
            for k, name, rows in ((B1, "cn_b1", C), (B2, "cn_b2", D2), (B3, "cn_b3", D3), (G1, "gc_b1", D2), (G2, "gc_b2", D3)):
                sp.dma_start(bias[0:rows, k:k + 1], io["L1_ffn_" + name].rearrange("(c o) -> c o", o=1)).then_inc(loaded, 16)
            for k, name in ((B4, "cn_b4"), (G3, "gc_b3"), (AR, "adaptive_range")):
                sp.dma_start(bias[:, k:k + 1], io["L1_ffn_" + name].rearrange("(o c) -> o c", o=1).broadcast_to([P, 1]))\
                  .then_inc(loaded, 16)

        LOADED = 16 * 15

        @block.gpsimd
        def _(pool):
            for n, a in enumerate((w3, w4, v2, v3, bias, g1, g2)):
                last = pool.memset(a[:, :], 0.0)
            last.then_inc(zeroed, 1)
            pool.memset(h2[:, :], 0.0)
            pool.memset(h3[:, :], 0.0).then_inc(prepared, 1)
            for t in range(B):
                pool.tensor_copy(out[:, cols(t)], S["xnT"][:, cols(t)]).then_inc(copied, 1)

        def item(n):
            return n % B

        @block.tensor
        def _(pe):
            pe.wait_ge(loaded, LOADED)
            pe.wait_ge(g_vec, 2)
            pe.matmul(misc[0:D2, 0:B], v1[:, :], context[:, :], start=True, stop=True).then_inc(g_mm, 1)
            pe.wait_ge(g_act, 1)
            pe.matmul(misc[0:D3, 16:16 + B], v2[:, :], g1[:, :], start=True, stop=True).then_inc(g_mm, 1)
            pe.wait_ge(g_act, 2)
            pe.matmul(misc[:, 32:32 + B], v3[:, 0:1].broadcast_to([P, P]), g2[:, :], start=True, stop=True).then_inc(g_mm, 1)
            pe.wait_ge(prepared, 1)

            def layer(s, n, t):
                if s == 0:
                    wait(pe, updated, n - B + 1)
                    if isinstance(n, int) and n < B:
                        wait(pe, copied, n + 1)
                    wait(pe, lay[0], n - 1)
                    pe.matmul(bank[t % 2][:, :], w1[:, :], out[:, cols(t)], start=True, stop=True).then_inc(mm[0], 1)
                elif s == 1:
                    wait(pe, lay[0], n + 1)
                    wait(pe, lay[1], n)
                    pe.matmul(quad[0:D2, 0, :], w2[:, :], h1[t % 2][:, :], start=True, stop=True).then_inc(mm[1], 1)
                elif s == 2:
                    wait(pe, lay[1], n + 1)
                    wait(pe, lay[2], n)
                    pe.matmul(quad[0:D3, 1, :], w3[:, :], h2[:, :], start=True, stop=True).then_inc(mm[2], 1)
                else:
                    wait(pe, lay[2], n + 1)
                    wait(pe, lay[3], n)
                    pe.matmul(quad[:, 2, :], w4[:, 0:1].broadcast_to([P, P]), h3[:, :], start=True, stop=True).then_inc(mm[3], 1)
                    wait(pe, delta_done, n)
                    pe.matmul(quad[:, 3, :], S["twist"], out[:, cols(t)], start=True, stop=True).then_inc(twisted, 1)

            def cycle(c, first):
                for k in range(B):
                    for s in range(4):
                        if not (first and k < s):
                            layer(s, c * B + k - s, item(k - s))

            cycle(0, True)
            with pe.Fori(1, CYCLES) as c:
                cycle(c, False)
            for k in range(3):
                for s in range(k + 1, 4):
                    layer(s, CYCLES * B + k - s, item(k - s))
            for t in range(B):
                pe.wait_ge(gated, t + 1)
                wait(pe, stored, t - 1)
                for m in range(TT):
                    last = pe.transpose(bank[t % 2][:, m * P:(m + 1) * P], gate[t % 2][:, m * P:(m + 1) * P], S["ident"])
                last.then_inc(turned, 1)

        @block.scalar
        def _(act):
            act.wait_ge(g_mm, 1)
            act.activation(g1[0:D2, :], misc[0:D2, 0:B], ACT.Gelu, bias=bias[0:D2, G1:G1 + 1]).then_inc(g_act, 1)
            act.wait_ge(g_mm, 2)
            act.activation(g2[0:D3, :], misc[0:D3, 16:16 + B], ACT.Gelu, bias=bias[0:D3, G2:G2 + 1]).then_inc(g_act, 1)
            act.wait_ge(g_mm, 3)
            act.wait_ge(g_vec, 3)
            act.activation(gt[:, :], misc[:, 32:32 + B], ACT.Tanh, bias=half[:, 1:2], scale=0.5).then_inc(g_act, 1)
            act.wait_ge(prepared, 1)

            def layer(s, n, t):
                wait(act, mm[s], n + 1)
                if s == 0:
                    wait(act, mm[1], n - 1)
                    act.activation(h1[t % 2][:, :], bank[t % 2][:, :], ACT.Gelu, bias=bias[:, B1:B1 + 1]).then_inc(lay[0], 1)
                elif s == 1:
                    wait(act, mm[2], n)
                    act.activation(h2[0:D2, :], quad[0:D2, 0, :], ACT.Gelu, bias=bias[0:D2, B2:B2 + 1]).then_inc(lay[1], 1)
                elif s == 2:
                    wait(act, mm[3], n)
                    act.activation(h3[0:D3, :], quad[0:D3, 1, :], ACT.Gelu, bias=bias[0:D3, B3:B3 + 1]).then_inc(lay[2], 1)
                else:
                    wait(act, coupled, n)
                    act.activation(tf[:, :], quad[:, 2, :], ACT.Tanh, bias=half[:, 0:1], scale=0.5).then_inc(lay[3], 1)

            def cycle(c, first):
                for k in range(B):
                    for s in range(4):
                        if not (first and k < s):
                            layer(s, c * B + k - s, item(k - s))

            cycle(0, True)
            with act.Fori(1, CYCLES) as c:
                cycle(c, False)
            for k in range(3):
                for s in range(k + 1, 4):
                    layer(s, CYCLES * B + k - s, item(k - s))
            for t in range(B):
                act.wait_ge(updated, (CYCLES - 1) * B + t + 1)
                wait(act, turned, t - 1)
                act.activation(gate[t % 2][:, :], out[:, cols(t)], ACT.Silu).then_inc(gated, 1)

        @block.vector
        def _(dve):
            for t in range(B):
                last = dve.tensor_reduce(means[:, t:t + 1], S["xnT"][:, cols(t)], AX_X, ALU.add)
            last.then_inc(g_vec, 1)
            dve.wait_ge(g_vec, 1)
            dve.tensor_scalar(context[:, :], means[:, :], 1.0 / T, None, ALU.mult).then_inc(g_vec, 1)
            dve.wait_ge(loaded, LOADED)
            dve.tensor_scalar(half[:, 0:1], bias[:, B4:B4 + 1], 0.5, None, ALU.mult)
            dve.tensor_scalar(half[:, 1:2], bias[:, G3:G3 + 1], 0.5, None, ALU.mult)
            dve.tensor_scalar(half[:, 2:3], bias[:, AR:AR + 1], 0.3, None, ALU.mult)
            dve.tensor_scalar(half[:, 3:4], bias[:, AR:AR + 1], 0.7, None, ALU.mult).then_inc(g_vec, 1)
            dve.wait_ge(g_vec, 3)
            dve.wait_ge(g_act, 3)
            dve.tensor_scalar(base[:, :], gt[:, :], half[:, 3:4], 0.1, ALU.mult, ALU.add).then_inc(g_vec, 1)
            dve.wait_ge(g_vec, 4)

            def update(n, t):
                wait(dve, lay[3], n + 1)
                wait(dve, delta_done, n)
                dve.tensor_scalar(coup[:, :], tf[:, :], half[:, 2:3], base[:, t:t + 1], ALU.mult, ALU.add).then_inc(coupled, 1)
                wait(dve, coupled, n + 1)
                wait(dve, twisted, n + 1)
                wait(dve, updated, n)
                dve.tensor_tensor(delta[:, :], coup[:, :], quad[:, 3, :], ALU.mult).then_inc(delta_done, 1)
                wait(dve, delta_done, n + 1)
                dve.tensor_tensor(out[:, cols(t)], out[:, cols(t)], delta[:, :], ALU.add).then_inc(updated, 1)

            for t in range(B):
                update(t, t)
            with dve.Fori(1, CYCLES) as c:
                for t in range(B):
                    update(c * B + t, t)
            for t in range(B):
                dve.wait_ge(turned, t + 1)
                dve.tensor_copy(S["s"][:, TT * t:TT * (t + 1), :], bank[t % 2][:, :].rearrange("p (m c) -> p m c", m=TT))\
                   .then_inc(stored, 1)


def attention1(nc, io, S):
    with ExitStack() as ctx:
        def sb(name, shape, dt=F32):
            return ctx.enter_context(nc.sbuf_tensor("a1_" + name, shape, dt))

        def sem(name):
            return ctx.enter_context(nc.semaphore("a1_" + name))

        xs = [sb(f"xs{i}", [C, T]) for i in range(2)]
        full = [sb(f"full{i}", [P, T]) for i in range(2)]
        rest = sb("rest", [P, T])
        parts = [sb(f"parts{i}", [P, 3, T], BF16) for i in range(4)]
        qs = [sb(f"qs{i}", [KROWS, H, T], BF16) for i in range(2)]
        ks = [sb(f"ks{i}", [KROWS, H, T], BF16) for i in range(2)]
        va = [sb(f"va{i}", [P, TT, H, STRIP]) for i in range(2)]
        vext = [sb(f"vext{i}", [P, TT, NCOMP]) for i in range(2)]
        probs = sb("probs", [P, 8, T])
        osb = [sb(f"osb{i}", [P, NG, T]) for i in range(2)]
        den = sb("den", [P, 2, H])
        rden = sb("rden", [P, 2, H])
        yn = sb("yn", [P, TT, C])
        yT = S["wT"]
        xg = sb("xg", [P, 2, TT, C])
        prod = yn
        so = sb("so", [P, TT, C])

        zeroed, filled = sem("zeroed"), sem("filled")
        xs_in, xg_in = sem("xs_in"), sem("xg_in")
        qk_mm, qk_read, qk_cast = sem("qk_mm"), sem("qk_read"), sem("qk_cast")
        rested, second, split = sem("rested"), sem("second"), sem("split")
        stack_a, stack_b = sem("stack_a"), sem("stack_b")
        v_mm, v_read = sem("v_mm"), sem("v_read")
        s_mm, squared, masked = sem("s_mm"), sem("squared"), sem("masked")
        av_mm, o_read = sem("av_mm"), sem("o_read")
        c_mm, floored, rec, yn_done = sem("c_mm"), sem("floored"), sem("rec"), sem("yn_done")
        yt_mm, yt_read = sem("yt_mm"), sem("yt_read")
        pr_mm, prod_done, so_done, so_out = sem("pr_mm"), sem("prod_done"), sem("so_done"), sem("so_out")
        quad, av, misc = S["quad"], S["av"], S["bank"][0]
        misc2 = S["bank"][1]
        block = ctx.enter_context(nc.Block())
        STACK = 16 * 2 * len(PAIRS)


        @block.sync
        def _(sp):
            def known(value):
                return value if isinstance(value, int) else sp.snap(sp.to_reg(value))

            def load_xs(b, par):
                col, mine, used, projected = known(b * T), known(16 * b), known(b - 1), known(4 * (b - 1))
                wait(sp, xs_in, mine)
                wait(sp, qk_mm, projected)
                wait(sp, v_mm, used)
                sp.dma_start(xs[par][:, :], S["xnT"][:, bass.ds(col, T)]).then_inc(xs_in, 16)

            def load_xg(b):
                tile0, mine, used = known(b * TT), known(32 * b), known(b)
                wait(sp, xg_in, mine)
                wait(sp, so_done, used)
                sp.dma_start(xg[:, 0], S["x"][:, bass.ds(tile0, TT), :]).then_inc(xg_in, 16)
                sp.dma_start(xg[:, 1], S["s"][:, bass.ds(tile0, TT), :]).then_inc(xg_in, 16)

            def stack(b, par, half):
                done = stack_b if half else stack_a
                split_now, scores_now, before = known(4 * b + 2 + 2 * half), known(64 * (b - 2) + 32 * (half + 1)), known(STACK * b)
                wait(sp, done, before)
                wait(sp, split, split_now)
                wait(sp, s_mm, scores_now)
                heads = slice(8 * half, 8 * half + 8)
                for n, (i, j) in enumerate(PAIRS):
                    for op, (dst, part) in enumerate(((qs, i), (ks, j))):
                        sp.dma_start(dst[par][DQ1 * n:DQ1 * (n + 1), heads, :], parts[2 * half + op][:, part, :]).then_inc(done, 16)

            def store(b):
                row, summed, before = known(b), known(b + 1), known(16 * b)
                wait(sp, so_out, before)
                wait(sp, so_done, summed)
                sp.dma_start(io["out"].rearrange("b (t p) c -> p b t c", p=P)[:, bass.ds(row, 1), :, :],
                             so[:, :, :]).then_inc(so_out, 16)

            def main(i, par, n):
                if n <= 5:
                    stack(i + 2, par, 0)
                if n >= 1:
                    store(i - 1)
                    load_xg(i)
                if n <= 4:
                    load_xs(i + 3, 1 - par)
                if n <= 5:
                    stack(i + 2, par, 1)

            load_xs(0, 0)
            load_xs(1, 1)
            load_xg(0)
            stack(0, 0, 0)
            stack(0, 0, 1)
            load_xs(2, 0)
            stack(1, 1, 0)
            stack(1, 1, 1)
            main(0, 0, 0)
            main(1, 1, 1)
            with sp.Fori(1, B // 2 - 2) as j:
                main(j * 2, 0, 2)
                main(j * 2 + 1, 1, 3)
            main(B - 4, 0, 4)
            main(B - 3, 1, 5)
            main(B - 2, 0, 6)
            main(B - 1, 1, 7)
            store(B - 1)
            sp.wait_ge(so_out, 16 * B)

        @block.gpsimd
        def _(pool):
            def split_one(c, k):
                f, r, pt = full[k % 2], rest, parts[k]
                wait(pool, qk_cast, c + 1)
                wait(pool, split, c)
                pool.tensor_tensor(r[:, :], f[:, :], pt[:, 0, :], ALU.subtract).then_inc(rested, 1)
                pool.tensor_tensor(pt[:, 1, :], f[:, :], pt[:, 0, :], ALU.subtract).then_inc(second, 1)
                wait(pool, rested, c + 1)
                wait(pool, second, c + 1)
                pool.tensor_tensor(pt[:, 2, :], r[:, :], pt[:, 1, :], ALU.subtract).then_inc(split, 1)

            for b in range(4):
                for k in range(4):
                    split_one(4 * b + k, k)
            with pool.Fori(1, B // 2 - 1) as j:
                for n in range(2):
                    for k in range(4):
                        split_one(8 * j + (4 * (n + 2) + k), k)

        @block.tensor
        def _(pe):
            def q_k(b, par, k):
                half, op = k // 2, k % 2
                if k == 0:
                    wait(pe, xs_in, 16 * (b + 1))
                w = S["wk1T"] if op else S["wq1T"]
                wait(pe, qk_read, 4 * b + k)
                pe.matmul(misc2[:, :], w[:, half * P:(half + 1) * P], xs[par][:, :], start=True, stop=True).then_inc(qk_mm, 1)

            def values(b, par):
                for t in range(TT):
                    last = pe.matmul(misc[:, t * P:(t + 1) * P], xs[par][:, t * P:(t + 1) * P], S["wv1T"],
                                     start=True, stop=True)
                last.then_inc(v_mm, 1)

            def score(b, par, t, j):
                g, kt = t // TT, t % TT
                h, n = GH * g + j, 4 * t + j
                if t == 0 and j == 0:
                    wait(pe, stack_a, STACK * (b + 1))
                if t == 8 and j == 0:
                    wait(pe, stack_b, STACK * (b + 1))
                wait(pe, squared, 64 * b + n - 3)
                pe.matmul(quad[:, n % 4, kt * P:T], ks[par][:, h, kt * P:(kt + 1) * P], qs[par][:, h, kt * P:T],
                          start=True, stop=True).then_inc(s_mm, 1)

            def weigh(b, par, t):
                g, kt = t // TT, t % TT
                wait(pe, masked, 64 * b + 4 * t + 4)
                if kt == 0:
                    wait(pe, o_read, 4 * b + g)
                if t == 0:
                    wait(pe, v_read, 2 * b + 2)
                for j in range(GH):
                    last = pe.matmul(av[STRIP * j:STRIP * (j + 1), kt * P:T], va[par][:, kt, GH * g + j, :],
                                     probs[:, (4 * t + j) % 8, kt * P:T], start=(kt == 0), stop=(kt == TT - 1))
                last.then_inc(av_mm, 1)

            def gather(b, par, pair):
                if pair == 0:
                    wait(pe, o_read, 4 * b + 4)
                for k in range(2):
                    t = 2 * pair + k
                    for kt in range(t + 1):
                        pe.matmul(misc[:, k * NCOMP:(k + 1) * NCOMP], S["tri"] if kt == t else S["ones"], vext[par][:, kt, :],
                                  start=(kt == 0), stop=False)
                    for g in range(NG):
                        last = pe.matmul(misc[:, k * NCOMP:(k + 1) * NCOMP], osb[par][:, g, t * P:(t + 1) * P],
                                         S["sel"][:, g * NCOMP:(g + 1) * NCOMP], start=False, stop=(g == NG - 1))
                last.then_inc(c_mm, 1)

            def finish_step(i, par, k):
                if k == 0:
                    gather(i, par, 0)
                elif k == 1:
                    wait(pe, yn_done, 2 * i + 1)
                    gather(i, par, 1)
                elif k == 2:
                    wait(pe, yn_done, 2 * i + 2)
                    for t in range(TT):
                        last = pe.transpose(misc[:, t * P:(t + 1) * P], yn[:, t, :], S["ident"])
                    last.then_inc(yt_mm, 1)
                else:
                    wait(pe, yt_read, i + 1)
                    for t in range(TT):
                        last = pe.matmul(misc[:, t * P:(t + 1) * P], yT[:, t * P:(t + 1) * P], S["wo1T"],
                                         start=True, stop=True)
                    last.then_inc(pr_mm, 1)

            def main(i, par, n):
                for t in range(STEPS):
                    for j in range(GH):
                        score(i, par, t, j)
                    if t >= 1:
                        weigh(i, par, t - 1)
                    elif n >= 1:
                        weigh(i - 1, 1 - par, STEPS - 1)
                    if n <= 5 and t in (1, 2, 11, 12):
                        q_k(i + 2, par, t - 1 if t < 8 else t - 9)
                    if 3 <= t <= 6 and n >= 1:
                        if t == 3:
                            wait(pe, v_read, 2 * i + 2)
                        finish_step(i - 1, 1 - par, t - 3)
                    if t == 7 and n <= 6:
                        wait(pe, prod_done, i) if n >= 1 else wait(pe, v_read, 2 * i + 2)
                        values(i + 1, 1 - par)

            for b in range(2):
                for k in range(4):
                    q_k(b, b, k)
                if b == 0:
                    values(0, 0)
            main(0, 0, 0)
            main(1, 1, 1)
            with pe.Fori(1, B // 2 - 1) as j:
                main(j * 2, 0, 2)
                main(j * 2 + 1, 1, 3)
            main(B - 2, 0, 6)
            main(B - 1, 1, 7)
            weigh(B - 1, 1, STEPS - 1)
            for k in range(4):
                if k == 0:
                    pe.wait_ge(prod_done, B - 1)
                finish_step(B - 1, 1, k)

        @block.scalar
        def _(act):
            def read_qk(b, k):
                half, op = k // 2, k % 2
                wait(act, qk_mm, 4 * b + k + 1)
                wait(act, split, 4 * b + k - 1)
                act.activation(full[op][:, :], misc2[:, :], ACT.Copy).then_inc(qk_read, 1)

            def squares(b, t):
                kt = t % TT
                for j in range(GH):
                    n = 4 * t + j
                    if j == 0:
                        wait(act, av_mm, 16 * b + t - 1)
                    wait(act, s_mm, 64 * b + n + 1)
                    act.activation(probs[:, n % 8, kt * P:T], quad[:, n % 4, kt * P:T], ACT.Square, bias=1.0, scale=0.25)\
                       .then_inc(squared, 1)

            def read_o(b, par, g):
                wait(act, av_mm, 16 * b + 4 * g + 4)
                wait(act, c_mm, 2 * (b - 1))
                act.activation(osb[par][:, g, :], av[:, :], ACT.Copy).then_inc(o_read, 1)

            def read_yT(b):
                wait(act, yt_mm, b + 1)
                wait(act, pr_mm, b)
                act.activation(yT[:, :], misc[:, :], ACT.Copy).then_inc(yt_read, 1)

            def main(i, par, n):
                for t in range(STEPS):
                    squares(i, t)
                    if t == 0 and n >= 1:
                        read_o(i - 1, 1 - par, NG - 1)
                    if t > 0 and t % TT == 0:
                        read_o(i, par, t // TT - 1)
                    if n <= 5 and t in (1, 2, 11, 12):
                        read_qk(i + 2, t - 1 if t < 8 else t - 9)
                    if t == 5 and n >= 1:
                        read_yT(i - 1)

            for b in range(2):
                for k in range(4):
                    read_qk(b, k)
            main(0, 0, 0)
            main(1, 1, 1)
            with act.Fori(1, B // 2 - 1) as j:
                main(j * 2, 0, 2)
                main(j * 2 + 1, 1, 3)
            main(B - 2, 0, 6)
            main(B - 1, 1, 7)
            read_o(B - 1, 1, NG - 1)
            read_yT(B - 1)

        @block.vector
        def _(dve):
            for i in range(2):
                dve.memset(va[i][:, :, :, :].bitcast(U32), 0).then_inc(zeroed, 1)
            for i in range(2):
                dve.memset(vext[i][:, :, C:NCOMP], 1.0)
            dve.wait_ge(zeroed, 2)
            for i in range(2):
                dve.memset(va[i][:, :, :, DH:DH + 1], 1.0).then_inc(filled, 1)
            dve.wait_ge(filled, 2)

            def cast(b, k):
                half, op = k // 2, k % 2
                wait(dve, qk_read, 4 * b + k + 1)
                wait(dve, stack_b if half else stack_a, STACK * b)
                dve.tensor_copy(parts[k][:, 0, :], full[op][:, :]).then_inc(qk_cast, 1)

            def mask(b, t):
                kt = t % TT
                for j in range(GH):
                    n = 4 * t + j
                    block_ = probs[:, n % 8, kt * P:(kt + 1) * P]
                    wait(dve, squared, 64 * b + n + 1)
                    dve.tensor_tensor(block_, block_, S["tri"], ALU.mult).then_inc(masked, 1)

            def read_v(b, par):
                wait(dve, v_mm, b + 1)
                wait(dve, av_mm, 16 * (b - 1))
                wait(dve, c_mm, 2 * (b - 1))
                dve.tensor_copy(va[par][:, :, :, 0:DH], misc[:, :].rearrange("p (t h d) -> p t h d", t=TT, d=DH)).then_inc(v_read, 1)
                dve.tensor_copy(vext[par][:, :, 0:C], misc[:, :].rearrange("p (t c) -> p t c", t=TT)).then_inc(v_read, 1)

            def divide(b, pair):
                c = 2 * b + pair + 1
                wait(dve, c_mm, c)
                m = misc[:, 0:2 * NCOMP].rearrange("p (k n) -> p k n", k=2)
                dve.tensor_scalar(den[:, :, :], m[:, :, C:NCOMP], 2 * EPS_L1, None, ALU.add).then_inc(floored, 1)
                wait(dve, floored, c)
                dve.reciprocal(rden[:, :, :], den[:, :, :]).then_inc(rec, 1)
                wait(dve, rec, c)
                if pair == 0:
                    wait(dve, so_done, b)
                dve.tensor_tensor(yn[:, 2 * pair:2 * pair + 2, :].rearrange("p k (h d) -> p k h d", d=DH),
                                  m[:, :, 0:C].rearrange("p k (h d) -> p k h d", d=DH),
                                  rden[:, :, :, None].broadcast_to([P, 2, H, DH]), ALU.mult).then_inc(yn_done, 1)

            def result(b):
                wait(dve, pr_mm, b + 1)
                wait(dve, xg_in, 32 * (b + 1))
                dve.tensor_tensor(prod[:, :, :], misc[:, :].rearrange("p (t c) -> p t c", t=TT), xg[:, 1], ALU.mult).then_inc(prod_done, 1)
                wait(dve, prod_done, b + 1)
                wait(dve, so_out, 16 * b)
                dve.tensor_tensor(so[:, :, :], prod[:, :, :], xg[:, 0], ALU.add).then_inc(so_done, 1)

            def main(i, par, n):
                for t in range(STEPS):
                    mask(i, t)
                    if n <= 5 and t in (1, 2, 11, 12):
                        cast(i + 2, t - 1 if t < 8 else t - 9)
                    if t in (3, 4) and n >= 1:
                        divide(i - 1, t - 3)
                    if t == 6 and n >= 1:
                        result(i - 1)
                    if t == 7 and n <= 6:
                        read_v(i + 1, 1 - par)

            for b in range(2):
                for k in range(4):
                    cast(b, k)
            read_v(0, 0)
            main(0, 0, 0)
            main(1, 1, 1)
            with dve.Fori(1, B // 2 - 1) as j:
                main(j * 2, 0, 2)
                main(j * 2 + 1, 1, 3)
            main(B - 2, 0, 6)
            main(B - 1, 1, 7)
            divide(B - 1, 0)
            divide(B - 1, 1)
            result(B - 1)


_INS = ["L0_attn_x", "L0_attn_Wq", "L0_attn_bq", "L0_attn_Wk", "L0_attn_bk", "L0_attn_Wv", "L0_attn_bv", "L0_attn_Wp",
        "L0_attn_bp", "L0_ffn_gate_w", "L0_ffn_w_gate", "L0_ffn_w_up", "L0_ffn_w_down", "L0_ffn_ws_gate",
        "L0_ffn_ws_up", "L0_ffn_ws_down", "L1_attn_Wq", "L1_attn_Wk", "L1_attn_Wv", "L1_attn_Wo", "L1_ffn_cn_w1",
        "L1_ffn_cn_b1", "L1_ffn_cn_w2", "L1_ffn_cn_b2", "L1_ffn_cn_w3", "L1_ffn_cn_b3", "L1_ffn_cn_w4",
        "L1_ffn_cn_b4", "L1_ffn_gc_w1", "L1_ffn_gc_b1", "L1_ffn_gc_w2", "L1_ffn_gc_b2", "L1_ffn_gc_w3",
        "L1_ffn_gc_b3", "L1_ffn_adaptive_range"]


def kernel(**inputs):
    import concourse.bacc as bacc
    from concourse.bass_utils import run_bass_kernel_spmd

    nc = bacc.Bacc("TRN2", target_bir_lowering=False, num_devices=1)
    arrays = {f"in_{name}": np.ascontiguousarray(inputs[name]) for name in _INS}
    arrays["in_shape_constants"] = shape_constants()
    io = {}
    for name, a in arrays.items():
        io[name[3:]] = nc.dram_tensor(name, a.shape, mybir.dt.from_np(a.dtype), kind="ExternalInput").ap()
    io["out"] = nc.dram_tensor("out_0", (B, T, C), F32, kind="ExternalOutput").ap()
    build_program(nc, io)
    r = run_bass_kernel_spmd(nc, [arrays], core_ids=[0])
    return r.results[0]["out_0"]
```

```python
from contextlib import ExitStack

import numpy as np

import concourse.bass as bass
from concourse import mybir

F32 = mybir.dt.float32
BF16 = mybir.dt.bfloat16
U32 = mybir.dt.uint32
ALU = mybir.AluOpType
ACT = mybir.ActivationFunctionType
AX_X = mybir.AxisListType.X

P = 128
C = 128
B, T = 8, 512
TT = T // P
NT = B * TT
H, DH = 16, 8
DQ1 = 16
GH = 4
NG = H // GH
STRIP = P // GH
NCOMP = C + H
STEPS = NG * TT
PAIRS = ((0, 0), (0, 1), (1, 0), (1, 1), (0, 2), (2, 0))
KROWS = 96
EPS_LN = 1e-5
EXPERTS, DFF = 8, 256
CHUNKS = DFF // P
EPS_L1 = 1e-12


def wait(engine, semaphore, count):
    if isinstance(count, int) and count <= 0:
        return
    engine.wait_ge(semaphore, count)


def shape_constants():
    ident = np.eye(P, dtype=np.float32)
    tri = np.triu(np.ones((P, P), np.float32))
    ones = np.ones((P, P), np.float32)
    sel = np.zeros((P, NG, NCOMP), np.float32)
    for g in range(NG):
        for j in range(GH):
            for d in range(DH):
                sel[STRIP * j + d, g, (GH * g + j) * DH + d] = 1.0
            sel[STRIP * j + DH, g, C + GH * g + j] = 1.0
    q = C // 4
    twist = np.zeros((P, P), np.float32)
    for i in range(q):
        twist[2 * q + i, i] = 1.0
        twist[3 * q + i, q + i] = -1.0
        twist[i, 2 * q + i] = -1.0
        twist[q + i, 3 * q + i] = 1.0
    lower = np.zeros((P, EXPERTS * EXPERTS), np.float32)
    lower[:] = np.tril(np.ones((EXPERTS, EXPERTS), np.float32), -1).ravel()
    return np.concatenate([ident, tri, ones, sel.reshape(P, -1), twist, lower], axis=1)


CONST_COLS = 3 * P + NG * NCOMP + P + EXPERTS * EXPERTS


def build_program(nc, io):
    with ExitStack() as whole:
        def keep(name, shape, dt=F32):
            return whole.enter_context(nc.sbuf_tensor(name, shape, dt))

        S = {}
        S["bank"] = [whole.enter_context(nc.psum_tensor(f"bank{i}", [P, T], F32)) for i in range(2)]
        S["quad"] = whole.enter_context(nc.psum_tensor("quad", [P, 4, T], F32))
        S["av"] = whole.enter_context(nc.psum_tensor("av", [P, T], F32))
        S["misc"] = whole.enter_context(nc.psum_tensor("misc", [P, T], F32))
        S["const"] = keep("const", [P, CONST_COLS])
        o = 0
        for name, n in (("ident", P), ("tri", P), ("ones", P), ("sel", NG * NCOMP), ("twist", P), ("lower", EXPERTS * EXPERTS)):
            S[name] = S["const"][:, o:o + n]
            o += n
        S["x"] = keep("x_tok", [P, NT, C])
        S["xnT"] = keep("xnT", [C, B * T])
        S["s"] = keep("s_tok", [P, NT, C])
        S["wT"] = keep("wT", [C, 4 * C])
        S["bqk"] = keep("bqk", [C, 2])
        S["bv"] = keep("bv", [P, C])
        S["bp"] = keep("bp", [P, C])
        S["w1T"] = keep("w1T", [C, 6 * C])
        for name, a, b in (("wq1T", 0, 2), ("wk1T", 2, 4), ("wv1T", 4, 5), ("wo1T", 5, 6)):
            S[name] = S["w1T"][:, a * C:b * C]
        S["gate"] = keep("gate", [C, EXPERTS])
        S["route"] = keep("route", [P, NT, EXPERTS])
        S["qs"] = [keep(f"q_stack{i}", [P, H, T], BF16) for i in range(2)]
        S["ks"] = [keep(f"k_stack{i}", [P, H, T], BF16) for i in range(2)]
        S["x_loaded"] = [whole.enter_context(nc.semaphore(f"x_loaded{c}")) for c in range(B)]
        prepare_weights(nc, io, S)
        layer_norm(nc, io, S, "ln0", S["x_loaded"])
        attention0(nc, io, S)
        moe(nc, io, S)
        layer_norm(nc, io, S, "ln1", None)
        coupling(nc, io, S)
        attention1(nc, io, S)


def prepare_weights(nc, io, S):
    names = ("Wq", "Wk", "Wv", "Wp")
    with ExitStack() as ctx:
        def sb(name, shape, dt=F32):
            return ctx.enter_context(nc.sbuf_tensor(name, shape, dt))

        def sem(name):
            return ctx.enter_context(nc.semaphore(name))

        w = sb("w_raw", [P, 4, C])
        w1 = sb("w1_raw", [P, 6, C])
        sign = sb("w_sign", [P, 4, C])
        diff = sb("w_diff", [P, 4, C])
        binary = sb("w_bin", [P, 4, C])
        scaled = sb("w_scaled", [P, 4, C])
        alpha = sb("w_alpha", [P, 8])
        loaded = sem("w_loaded")
        loaded1 = sem("w1_loaded")
        small = sem("w_small_loaded")
        signed = sem("w_signed")
        summed = sem("w_summed")
        meaned = sem("w_meaned")
        differed = sem("w_differed")
        rebuilt = sem("w_rebuilt")
        multiplied = sem("w_multiplied")
        turned = sem("w_turned")
        copied = sem("w_copied")
        cleared = sem("w_stacks_cleared")
        block = ctx.enter_context(nc.Block())

        @block.sync
        def _(sp):
            sp.dma_start(S["const"][:, :], io["shape_constants"]).then_inc(loaded, 16)
            for n, name in enumerate(names):
                if n >= 2:
                    sp.dma_start(w[:, n, :], io["L0_attn_" + name]).then_inc(loaded, 32)
                    continue
                for f in range(2):
                    rows = slice(64 * f, 64 * (f + 1))
                    sp.dma_start(w[rows, n, :], io["L0_attn_" + name][rows, :].rearrange("(h d) c -> d h c", d=DH))\
                      .then_inc(loaded, 16)
                    sp.dma_start(S["bqk"][rows, n:n + 1],
                                 io["L0_attn_bq" if n == 0 else "L0_attn_bk"][rows].rearrange("(h d o) -> d h o", d=DH, o=1),
                                 allow_slow_non_contiguous=True)\
                      .then_inc(small, 16)
            sp.dma_start(S["gate"][:, :], io["L0_ffn_gate_w"]).then_inc(small, 16)
            sp.dma_start(S["bv"][:, :], io["L0_attn_bv"].rearrange("(o c) -> o c", o=1).broadcast_to([P, C])).then_inc(small, 16)
            sp.dma_start(S["bp"][:, :], io["L0_attn_bp"].rearrange("(o c) -> o c", o=1).broadcast_to([P, C])).then_inc(small, 16)
            for n, name in enumerate(("Wq", "Wk")):
                for k in range(2):
                    src = io["L1_attn_" + name][k * P:(k + 1) * P, :].rearrange("(h d) c -> d h c", d=DQ1)
                    sp.dma_start(w1[:, 2 * n + k, :], src).then_inc(loaded1, 16)
            for n, name in enumerate(("Wv", "Wo")):
                sp.dma_start(w1[:, 4 + n, :], io["L1_attn_" + name]).then_inc(loaded1, 16)
            xv = io["L0_attn_x"].rearrange("b (t p) c -> b p t c", p=P)
            for c in range(B):
                sp.dma_start(S["x"][:, TT * c:TT * (c + 1), :], xv[c]).then_inc(S["x_loaded"][c], 16)
            sp.wait_ge(small, 16 * 7)

        @block.gpsimd
        def _(pool):
            for tensor in (S["qs"][0], S["ks"][0]):
                pool.memset(tensor[:, :, :].bitcast(U32), 0).then_inc(cleared, 1)
            pool.wait_ge(cleared, 4)
            for tensor in S["ks"]:
                pool.memset(tensor[KROWS:KROWS + 3, :, :], 1.0)

        @block.scalar
        def _(act):
            act.wait_ge(loaded, 16 * 9)
            act.activation(sign[:, :, :], w[:, :, :], ACT.Sign).then_inc(signed, 1)
            act.wait_ge(turned, 1)
            act.activation(S["w1T"][:, 0:T], S["quad"][:, 0, :], ACT.Copy)
            act.activation(S["w1T"][:, T:], S["quad"][:, 1, 0:2 * P], ACT.Copy)
            act.wait_ge(turned, 2)
            act.activation(S["wT"][:, :], S["misc"][:, :], ACT.Copy).then_inc(copied, 1)

        @block.vector
        def _(dve):
            for tensor in (S["qs"][1], S["ks"][1]):
                dve.memset(tensor[:, :, :].bitcast(U32), 0).then_inc(cleared, 1)
            dve.wait_ge(loaded, 16 * 9)
            dve.tensor_reduce(alpha[:, 0:4], w[:, :, :], AX_X, ALU.add, apply_absolute_value=True).then_inc(summed, 1)
            dve.wait_ge(signed, 1)
            dve.tensor_tensor(diff[:, :, :], sign[:, :, :], w[:, :, :], ALU.subtract).then_inc(differed, 1)
            dve.wait_ge(summed, 1)
            dve.tensor_scalar(alpha[:, 4:8], alpha[:, 0:4], 1.0 / C, None, ALU.mult).then_inc(meaned, 1)
            dve.wait_ge(differed, 1)
            dve.tensor_tensor(binary[:, :, :], w[:, :, :], diff[:, :, :], ALU.add).then_inc(rebuilt, 1)
            dve.wait_ge(rebuilt, 1)
            dve.wait_ge(meaned, 1)
            dve.tensor_tensor(scaled[:, :, :], binary[:, :, :], alpha[:, 4:8, None].broadcast_to([P, 4, C]), ALU.mult).then_inc(multiplied, 1)

        @block.tensor
        def _(pe):
            pe.wait_ge(loaded, 16 * 9)
            pe.wait_ge(loaded1, 16 * 6)
            for n in range(6):
                last = pe.transpose(S["quad"][:, n // 4, (n % 4) * P:(n % 4 + 1) * P], w1[:, n, :], S["ident"])
            last.then_inc(turned, 1)
            pe.wait_ge(multiplied, 1)
            for n in range(4):
                last = pe.transpose(S["misc"][:, n * P:(n + 1) * P], scaled[:, n, :], S["ident"])
            last.then_inc(turned, 1)


def layer_norm(nc, io, S, tag, loaded):
    x, xnT = S["x"], S["xnT"]
    with ExitStack() as ctx:
        def sb(name, shape, dt=F32):
            return ctx.enter_context(nc.sbuf_tensor(f"{tag}_{name}", shape, dt))

        def sem(name):
            return ctx.enter_context(nc.semaphore(f"{tag}_{name}"))

        xc = sb("normalised", [P, NT, C])
        stats = sb("stats", [P, NT, 6])
        mean_var = sb("mean_var", [P, NT, 2])
        vare = sb("vare", [P, NT])
        std = sb("std", [P, NT])
        rstd = sb("rstd", [P, NT])
        measured = sem("measured")
        joined = sem("joined")
        shifted = sem("shifted")
        rooted = sem("rooted")
        inverted = sem("inverted")
        scaled = sem("scaled")
        turned = sem("turned")
        stored = sem("stored")
        block = ctx.enter_context(nc.Block())

        def tiles(c):
            return slice(TT * c, TT * (c + 1))

        @block.vector
        def _(dve):
            for c in range(B + 1):
                if c < B:
                    if loaded is not None:
                        dve.wait_ge(loaded[c], 16)
                    for t in range(TT * c, TT * (c + 1)):
                        last = dve.bn_stats(out=stats[:, t, :], in_=x[:, t, :])
                    last.then_inc(measured, 1)
                if c >= 1:
                    dve.wait_ge(rooted, c)
                    dve.reciprocal(rstd[:, tiles(c - 1)], std[:, tiles(c - 1)]).then_inc(inverted, 1)
                if c < B:
                    dve.wait_ge(measured, c + 1)
                    for t in range(TT * c, TT * (c + 1)):
                        last = dve.bn_aggr(out=mean_var[:, t, :], in_=stats[:, t, :])
                    last.then_inc(joined, 1)
                    dve.wait_ge(joined, c + 1)
                    dve.tensor_scalar(vare[:, tiles(c)], mean_var[:, tiles(c), 1], EPS_LN, None, ALU.add).then_inc(shifted, 1)
                if c >= 1:
                    dve.wait_ge(inverted, c)
                    for t in range(TT * (c - 1), TT * c):
                        last = dve.tensor_scalar(xc[:, t, :], x[:, t, :], mean_var[:, t, 0:1], rstd[:, t:t + 1],
                                                 ALU.subtract, ALU.mult)
                    last.then_inc(scaled, 1)

        @block.scalar
        def _(act):
            def store(c):
                act.wait_ge(turned, c + 1)
                act.activation(xnT[:, T * c:T * (c + 1)], S["bank"][c % 2][:, :], ACT.Copy).then_inc(stored, 1)

            for c in range(B):
                act.wait_ge(shifted, c + 1)
                act.activation(std[:, tiles(c)], vare[:, tiles(c)], ACT.Sqrt).then_inc(rooted, 1)
                if c >= 2:
                    store(c - 2)
            store(B - 2)
            store(B - 1)

        @block.tensor
        def _(pe):
            for c in range(B):
                pe.wait_ge(scaled, c + 1)
                if c >= 2:
                    pe.wait_ge(stored, c - 1)
                for t in range(TT):
                    last = pe.transpose(S["bank"][c % 2][:, t * P:(t + 1) * P], xc[:, TT * c + t, :], S["ident"])
                last.then_inc(turned, 1)


def attention0(nc, io, S):
    scale = DH ** -0.5
    with ExitStack() as ctx:
        def sb(name, shape, dt=F32):
            return ctx.enter_context(nc.sbuf_tensor("a0_" + name, shape, dt))

        def sem(name):
            return ctx.enter_context(nc.semaphore("a0_" + name))

        xs = [sb(f"xs{i}", [C, T]) for i in range(2)]
        full = [sb(f"full{i}", [P, T]) for i in range(2)]
        rest = [sb(f"rest{i}", [P, T]) for i in range(2)]
        parts = [sb(f"parts{i}", [P, 3, T], BF16) for i in range(2)]
        qs, ks = S["qs"], S["ks"]
        va = [sb(f"va{i}", [P, TT, H, STRIP]) for i in range(2)]
        probs = sb("probs", [P, 8, T])
        osb = [sb(f"osb{i}", [P, NG, T]) for i in range(2)]
        nmax = [sb(f"nmax{i}", [P, P]) for i in range(2)]
        nrest = sb("nrest", [STRIP, P])
        nparts = sb("nparts", [STRIP, 3, P], BF16)
        rden = sb("rden", [P, 2, H])
        yn = sb("yn", [P, TT, C])
        yT = sb("yT", [C, T])
        so = sb("so", [P, TT, C])

        xs_in = sem("xs_in")
        q_mm, k_mm, v_mm = sem("q_mm"), sem("k_mm"), sem("v_mm")
        qk_read = sem("qk_read")
        rested = sem("rested")
        second = sem("second")
        split = sem("split")
        stack_a, stack_b = sem("stack_a"), sem("stack_b")
        v_read = sem("v_read")
        max_mm, max_red = sem("max_mm"), sem("max_red")
        nm_mm = sem("nm_mm")
        n0, n1, n2 = sem("n0"), sem("n1"), sem("n2")
        ns_done = sem("ns_done")
        mrows = sem("mrows")
        s_mm, exped = sem("s_mm"), sem("exped")
        av_mm, o_read = sem("av_mm"), sem("o_read")
        c_mm, rec, yn_done = sem("c_mm"), sem("rec"), sem("yn_done")
        yt_mm, yt_read = sem("yt_mm"), sem("yt_read")
        pr_mm, so_done, so_out = sem("pr_mm"), sem("so_done"), sem("so_out")
        bank, quad, av, misc = S["bank"], S["quad"], S["av"], S["misc"]
        wT = S["wT"]

        E = EXPERTS
        logits = av[:, 0:NT * E].rearrange("p (t e) -> p t e", e=E)
        room = probs[:, :, :].rearrange("p s t -> p (s t)")
        shifted, expo, prob, rank, chosen = (room[:, NT * E * i:NT * E * (i + 1)].rearrange("p (t e) -> p t e", e=E)
                                             for i in range(5))
        top, total, inv, norm = (room[:, NT * (5 * E + i):NT * (5 * E + i + 1)] for i in range(4))
        above, level = (o[:, :, :].rearrange("p g (t e j) -> p (g t) e j", e=E, j=E) for o in osb)
        r_scored, route_step, r_exponents = sem("route_scored"), sem("route_step"), sem("route_exponents")
        block = ctx.enter_context(nc.Block())

        STACK = 16 * 2 * len(PAIRS)


        @block.sync
        def _(sp):
            def known(value):
                return value if isinstance(value, int) else sp.snap(sp.to_reg(value))

            def load_xs(b, par, col):
                col = known(col)
                mine, used = known(16 * b), known(b - 1)
                wait(sp, xs_in, mine)
                wait(sp, v_mm, used)
                sp.dma_start(xs[par][:, :], S["xnT"][:, bass.ds(col, T)]).then_inc(xs_in, 16)

            def stack(b, par, half):
                done = stack_b if half else stack_a
                split_now, scores_now, before = known(2 * b + 2), known(64 * (b - 2) + 32 * (half + 1)), known(STACK * b)
                wait(sp, done, before)
                wait(sp, split, split_now)
                wait(sp, s_mm, scores_now)
                rows = slice(64 * half, 64 * half + 64)
                heads = slice(8 * half, 8 * half + 8)
                for n, (i, j) in enumerate(PAIRS):
                    for op, (dst, part) in enumerate(((qs, i), (ks, j))):
                        src = parts[op][rows, part, :]
                        sp.dma_start(dst[par][DH * n:DH * (n + 1), heads, :], src).then_inc(done, 16)

            def max_rows(b, par, half):
                split_now, before = known(2 * b + half + 1), known(48 * (2 * b + half))
                wait(sp, mrows, before)
                wait(sp, ns_done, split_now)
                for i in range(3):
                    sp.dma_start(qs[par][KROWS + i:KROWS + i + 1, 8 * half:8 * half + 8, :],
                                 nparts[:, i, :]).then_inc(mrows, 16)

            def store_s(b, tile0):
                tile0, summed, before = known(tile0), known(b + 1), known(16 * b)
                wait(sp, so_out, before)
                wait(sp, so_done, summed)
                sp.dma_start(S["s"][:, bass.ds(tile0, TT), :], so[:, :, :]).then_inc(so_out, 16)

            def main(i, par, n):
                max_rows(i, par, 1)
                if n <= 5:
                    stack(i + 2, par, 0)
                if n <= 4:
                    load_xs(i + 3, 1 - par, (i + 3) * T)
                if n >= 1:
                    store_s(i - 1, (i - 1) * TT)
                if n <= 6:
                    max_rows(i + 1, 1 - par, 0)
                if n <= 5:
                    stack(i + 2, par, 1)

            load_xs(0, 0, 0)
            load_xs(1, 1, T)
            stack(0, 0, 0)
            stack(0, 0, 1)
            load_xs(2, 0, 2 * T)
            stack(1, 1, 0)
            stack(1, 1, 1)
            max_rows(0, 0, 0)
            main(0, 0, 0)
            main(1, 1, 1)
            with sp.Fori(1, B // 2 - 2) as j:
                main(j * 2, 0, 2)
                main(j * 2 + 1, 1, 3)
            main(B - 4, 0, 4)
            main(B - 3, 1, 5)
            main(6, 0, 6)
            main(7, 1, 7)
            store_s(7, 7 * TT)
            sp.wait_ge(so_out, 16 * B)

        @block.gpsimd
        def _(pool):
            def split_one(b, op):
                f, r, pt = full[op], rest[op], parts[op]
                wait(pool, qk_read, 2 * b + op + 1)
                pool.tensor_tensor(r[:, :], f[:, :], pt[:, 0, :], ALU.subtract).then_inc(rested, 1)
                pool.tensor_tensor(pt[:, 1, :], f[:, :], pt[:, 0, :], ALU.subtract).then_inc(second, 1)
                wait(pool, rested, 2 * b + op + 1)
                wait(pool, second, 2 * b + op + 1)
                pool.tensor_tensor(pt[:, 2, :], r[:, :], pt[:, 1, :], ALU.subtract).then_inc(split, 1)

            for b in range(2):
                for op in range(2):
                    split_one(b, op)
            for i in range(2):
                for op in range(2):
                    split_one(i + 2, op)
            with pool.Fori(1, 3) as j:
                for n in range(2):
                    for op in range(2):
                        split_one(j * 2 + n + 2, op)

        @block.tensor
        def _(pe):
            def q_k(b, par, op):
                if op == 0:
                    wait(pe, xs_in, 16 * (b + 1))
                pe.matmul(misc[:, :], wT[:, op * C:(op + 1) * C], xs[par][:, :], start=True, stop=True)\
                  .then_inc(k_mm if op else q_mm, 1)

            def values(b, par):
                for t in range(TT):
                    last = pe.matmul(misc[:, t * P:(t + 1) * P], xs[par][:, t * P:(t + 1) * P], wT[:, 2 * C:3 * C],
                                     start=True, stop=True)
                last.then_inc(v_mm, 1)

            def max_tile(b, par, u):
                h, qt = u // TT, u % TT
                if u == 0:
                    wait(pe, stack_a, STACK * (b + 1))
                if u == 32:
                    wait(pe, stack_b, STACK * (b + 1))
                if u % 2 == 0:
                    wait(pe, max_red, 32 * b + u // 2 - 1)
                mm = pe.matmul(quad[:, 2 * ((u // 2) % 2) + u % 2, :], qs[par][0:KROWS, h, qt * P:(qt + 1) * P],
                               ks[par][0:KROWS, h, :], start=True, stop=True)
                if u % 2:
                    mm.then_inc(max_mm, 1)

            def max_turn(b, half):
                wait(pe, max_red, 32 * b + 16 * (half + 1))
                pe.transpose(misc[:, 0:P], nmax[half][:, :], S["ident"]).then_inc(nm_mm, 1)

            def score(b, par, t, j):
                g, kt = t // TT, t % TT
                h, n = GH * g + j, 4 * t + j
                if t == 0 and j == 0:
                    wait(pe, mrows, 96 * b + 48)
                if t == 8 and j == 0:
                    wait(pe, mrows, 96 * b + 96)
                wait(pe, exped, 64 * b + n - 1)
                pe.matmul(bank[n % 2][:, :], ks[par][0:KROWS + 3, h, kt * P:(kt + 1) * P], qs[par][0:KROWS + 3, h, :],
                          start=True, stop=True).then_inc(s_mm, 1)

            def weigh(b, par, t):
                g, kt = t // TT, t % TT
                wait(pe, exped, 64 * b + 4 * t + 4)
                if kt == 0:
                    wait(pe, o_read, 4 * b + g)
                if t == 0:
                    wait(pe, v_read, b + 1)
                for j in range(GH):
                    last = pe.matmul(av[STRIP * j:STRIP * (j + 1), :], va[par][:, kt, GH * g + j, :],
                                     probs[:, (4 * t + j) % 8, :], start=(kt == 0), stop=(kt == TT - 1))
                last.then_inc(av_mm, 1)

            def gather(b, par, pair):
                if pair == 0:
                    wait(pe, o_read, 4 * b + 4)
                for k in range(2):
                    t = 2 * pair + k
                    for g in range(NG):
                        last = pe.matmul(misc[:, k * NCOMP:(k + 1) * NCOMP], osb[par][:, g, t * P:(t + 1) * P],
                                         S["sel"][:, g * NCOMP:(g + 1) * NCOMP], start=(g == 0), stop=(g == NG - 1))
                last.then_inc(c_mm, 1)

            def turn_y(b):
                wait(pe, yn_done, 2 * b + 2)
                for t in range(TT):
                    last = pe.transpose(misc[:, t * P:(t + 1) * P], yn[:, t, :], S["ident"])
                last.then_inc(yt_mm, 1)

            def project(b):
                wait(pe, yt_read, b + 1)
                for t in range(TT):
                    last = pe.matmul(misc[:, t * P:(t + 1) * P], yT[:, t * P:(t + 1) * P], wT[:, 3 * C:4 * C],
                                     start=True, stop=True)
                last.then_inc(pr_mm, 1)

            def finish_step(i, par, k, n):
                if k == 0:
                    gather(i, par, 0)
                elif k == 1:
                    wait(pe, yn_done, 2 * i + 1)
                    gather(i, par, 1)
                elif k == 2:
                    turn_y(i)
                else:
                    project(i)

            def main(i, par, n):
                for t in range(STEPS):
                    for j in range(GH):
                        if j == GH // 2:
                            if t >= 1:
                                weigh(i, par, t - 1)
                            elif n >= 1:
                                weigh(i - 1, 1 - par, STEPS - 1)
                        score(i, par, t, j)
                        if n <= 6:
                            max_tile(i + 1, 1 - par, 4 * t + j)
                    if t == 1:
                        wait(pe, so_done, i - 1)
                        wait(pe, ns_done, 2 * i + 1)
                        max_turn(i, 1)
                    if t == 2 and n <= 5:
                        wait(pe, ns_done, 2 * i + 2)
                        q_k(i + 2, par, 0)
                    if t == 3 and n <= 5:
                        wait(pe, qk_read, 2 * i + 5)
                        q_k(i + 2, par, 1)
                    if t == 4 and n <= 6:
                        wait(pe, qk_read, 2 * i + 6) if n <= 5 else wait(pe, ns_done, 2 * i + 2)
                        values(i + 1, 1 - par)
                    if 5 <= t <= 8 and n >= 1:
                        if t == 5:
                            wait(pe, v_read, i + 2) if n <= 6 else wait(pe, ns_done, 2 * i + 2)
                        finish_step(i - 1, 1 - par, t - 5, n)
                    if t == 9 and n <= 6:
                        wait(pe, so_done, i) if n >= 1 else wait(pe, v_read, i + 2)
                        max_turn(i + 1, 0)

            q_k(0, 0, 0)
            pe.wait_ge(qk_read, 1)
            q_k(0, 0, 1)
            for t in range(NT):
                last = pe.matmul(av[:, E * t:E * (t + 1)], S["xnT"][:, P * t:P * (t + 1)], S["gate"][:, :],
                                 start=True, stop=True)
            last.then_inc(r_scored, 1)
            pe.wait_ge(qk_read, 2)
            q_k(1, 1, 0)
            pe.wait_ge(qk_read, 3)
            q_k(1, 1, 1)
            pe.wait_ge(qk_read, 4)
            values(0, 0)
            for u in range(4 * STEPS):
                max_tile(0, 0, u)
            pe.wait_ge(v_read, 1)
            max_turn(0, 0)
            main(0, 0, 0)
            main(1, 1, 1)
            with pe.Fori(1, 3) as j:
                main(j * 2, 0, 2)
                main(j * 2 + 1, 1, 3)
            main(6, 0, 6)
            main(7, 1, 7)
            weigh(7, 1, STEPS - 1)
            pe.wait_ge(so_done, 7)
            for k in range(4):
                finish_step(7, 1, k, 8)

        @block.scalar
        def _(act):
            def read_qk(b, op):
                wait(act, k_mm if op else q_mm, b + 1)
                wait(act, stack_b, STACK * b)
                wait(act, split, 2 * b - 1 + op)
                act.activation(full[op][:, :], misc[:, :], ACT.Identity, bias=S["bqk"][:, op:op + 1])
                act.activation(parts[op][:, 0, :], misc[:, :], ACT.Identity, bias=S["bqk"][:, op:op + 1])\
                   .then_inc(qk_read, 1)

            def exps(b, t):
                for j in range(GH):
                    n = 4 * t + j
                    if j == 0:
                        wait(act, av_mm, 16 * b + t - 1)
                    wait(act, s_mm, 64 * b + n + 1)
                    act.activation(probs[:, n % 8, :], bank[n % 2][:, :], ACT.Exp, scale=scale).then_inc(exped, 1)

            def read_o(b, par, g):
                wait(act, av_mm, 16 * b + 4 * g + 4)
                wait(act, c_mm, 2 * (b - 1))
                act.activation(osb[par][:, g, :], av[:, :], ACT.Copy).then_inc(o_read, 1)

            def read_yT(b):
                wait(act, yt_mm, b + 1)
                wait(act, pr_mm, b)
                act.activation(yT[:, :], misc[:, :], ACT.Copy).then_inc(yt_read, 1)

            def main(i, par, n):
                for t in range(STEPS):
                    exps(i, t)
                    if t == 0 and n >= 1:
                        read_o(i - 1, 1 - par, NG - 1)
                    if t > 0 and t % TT == 0:
                        read_o(i, par, t // TT - 1)
                    if t == 2 and n <= 5:
                        read_qk(i + 2, 0)
                    if t == 3 and n <= 5:
                        read_qk(i + 2, 1)
                    if t == 7 and n >= 1:
                        read_yT(i - 1)

            for b in range(2):
                for op in range(2):
                    read_qk(b, op)
                if b == 0:
                    act.wait_ge(route_step, 2)
                    act.activation(expo, shifted, ACT.Exp).then_inc(r_exponents, 1)
            main(0, 0, 0)
            main(1, 1, 1)
            with act.Fori(1, 3) as j:
                main(j * 2, 0, 2)
                main(j * 2 + 1, 1, 3)
            main(6, 0, 6)
            main(7, 1, 7)
            read_o(7, 1, NG - 1)
            read_yT(7)

        @block.vector
        def _(dve):
            for i in range(2):
                dve.memset(va[i][:, :, :, :].bitcast(U32), 0).then_inc(n0, 1)
                dve.memset(nmax[i][:, :], 0.0)
            dve.wait_ge(n0, 2)
            for i in range(2):
                dve.memset(va[i][:, :, :, DH:DH + 1], 1.0)

            def read_v(b, par):
                wait(dve, v_mm, b + 1)
                wait(dve, av_mm, 16 * (b - 1))
                dve.tensor_tensor(va[par][:, :, :, 0:DH], misc[:, :].rearrange("p (t h d) -> p t h d", t=TT, d=DH),
                                  S["bv"][:, None, :].broadcast_to([P, TT, C]).rearrange("p t (h d) -> p t h d", d=DH),
                                  ALU.add).then_inc(v_read, 1)

            def maxima(b, w):
                half = w // 16
                if w % 16 == 0:
                    wait(dve, nm_mm, 2 * b - 1 + half)
                wait(dve, max_mm, 32 * b + w + 1)
                dve.tensor_reduce(nmax[half][:, 2 * (w % 16):2 * (w % 16) + 2], quad[:, 2 * (w % 2):2 * (w % 2) + 2, :],
                                  AX_X, ALU.max, negate=True).then_inc(max_red, 1)

            def split_max(b, half):
                c = 2 * b + half + 1
                wait(dve, nm_mm, c)
                wait(dve, mrows, 48 * (c - 1))
                m = misc[0:STRIP, 0:P]
                dve.tensor_copy(nparts[:, 0, :], m).then_inc(n1, 1)
                wait(dve, n1, c)
                dve.tensor_tensor(nrest[:, :], m, nparts[:, 0, :], ALU.subtract)
                dve.tensor_tensor(nparts[:, 1, :], m, nparts[:, 0, :], ALU.subtract).then_inc(n2, 1)
                wait(dve, n2, c)
                dve.tensor_tensor(nparts[:, 2, :], nrest[:, :], nparts[:, 1, :], ALU.subtract).then_inc(ns_done, 1)

            def divide(b, pair):
                c = 2 * b + pair + 1
                wait(dve, c_mm, c)
                m = misc[:, 0:2 * NCOMP].rearrange("p (k n) -> p k n", k=2)
                dve.reciprocal(rden[:, :, :], m[:, :, C:NCOMP]).then_inc(rec, 1)
                wait(dve, rec, c)
                if pair == 0:
                    wait(dve, yt_mm, b)
                dve.tensor_tensor(yn[:, 2 * pair:2 * pair + 2, :].rearrange("p k (h d) -> p k h d", d=DH),
                                  m[:, :, 0:C].rearrange("p k (h d) -> p k h d", d=DH),
                                  rden[:, :, :, None].broadcast_to([P, 2, H, DH]), ALU.mult).then_inc(yn_done, 1)

            def read_s(b):
                wait(dve, pr_mm, b + 1)
                wait(dve, so_out, 16 * b)
                dve.tensor_tensor(so[:, :, :], misc[:, :].rearrange("p (t c) -> p t c", t=TT),
                                  S["bp"][:, None, :].broadcast_to([P, TT, C]), ALU.add).then_inc(so_done, 1)

            def route_weights():
                def over(a):
                    return a[:, :, None].broadcast_to([P, NT, E])

                dve.wait_ge(r_scored, 1)
                dve.tensor_reduce(top[:, :], logits, AX_X, ALU.max).then_inc(route_step, 1)
                dve.wait_ge(route_step, 1)
                dve.tensor_tensor(shifted[:, :, :], logits, over(top), ALU.subtract).then_inc(route_step, 1)
                dve.wait_ge(r_exponents, 1)
                dve.tensor_reduce(total[:, :], expo[:, :, :], AX_X, ALU.add).then_inc(route_step, 1)
                dve.wait_ge(route_step, 3)
                dve.reciprocal(inv[:, :], total[:, :]).then_inc(route_step, 1)
                dve.wait_ge(route_step, 4)
                dve.tensor_tensor(prob[:, :, :], expo[:, :, :], over(inv), ALU.mult).then_inc(route_step, 1)
                dve.wait_ge(route_step, 5)
                other = prob[:, :, None, :].broadcast_to([P, NT, E, E])
                own = prob[:, :, :, None].broadcast_to([P, NT, E, E])
                dve.tensor_tensor(above[:, :, :, :], other, own, ALU.is_gt)
                dve.tensor_tensor(level[:, :, :, :], other, own, ALU.is_ge).then_inc(route_step, 1)
                dve.wait_ge(route_step, 6)
                lower = S["lower"].rearrange("p (o e j) -> p o e j", o=1, e=E).broadcast_to([P, NT, E, E])
                dve.tensor_tensor(level[:, :, :, :], level[:, :, :, :], lower, ALU.mult).then_inc(route_step, 1)
                dve.wait_ge(route_step, 7)
                dve.tensor_tensor(level[:, :, :, :], level[:, :, :, :], above[:, :, :, :], ALU.max).then_inc(route_step, 1)
                dve.wait_ge(route_step, 8)
                dve.tensor_reduce(rank[:, :, :], level[:, :, :, :], AX_X, ALU.add).then_inc(route_step, 1)
                dve.wait_ge(route_step, 9)
                dve.scalar_tensor_tensor(out=chosen[:, :, :], in0=rank[:, :, :], scalar=1.5, in1=prob[:, :, :],
                                         op0=ALU.is_lt, op1=ALU.mult).then_inc(route_step, 1)
                dve.wait_ge(route_step, 10)
                dve.tensor_reduce(norm[:, :], chosen[:, :, :], AX_X, ALU.add).then_inc(route_step, 1)
                dve.wait_ge(route_step, 11)
                dve.tensor_scalar(top[:, :], norm[:, :], 1e-20, None, ALU.add).then_inc(route_step, 1)
                dve.wait_ge(route_step, 12)
                dve.reciprocal(inv[:, :], top[:, :]).then_inc(route_step, 1)
                dve.wait_ge(route_step, 13)
                dve.tensor_tensor(S["route"][:, :, :], chosen[:, :, :], over(inv), ALU.mult).then_inc(route_step, 1)

            def main(i, par, n):
                for t in range(STEPS):
                    if n <= 6:
                        maxima(i + 1, 2 * t)
                        maxima(i + 1, 2 * t + 1)
                    if t == 1:
                        split_max(i, 1)
                    if t == 4 and n <= 6:
                        read_v(i + 1, 1 - par)
                    if t in (5, 6) and n >= 1:
                        divide(i - 1, t - 5)
                    if t == 8 and n >= 1:
                        read_s(i - 1)
                    if t == 9 and n <= 6:
                        split_max(i + 1, 0)

            route_weights()
            read_v(0, 0)
            for w in range(2 * STEPS):
                maxima(0, w)
            split_max(0, 0)
            main(0, 0, 0)
            main(1, 1, 1)
            with dve.Fori(1, 3) as j:
                main(j * 2, 0, 2)
                main(j * 2 + 1, 1, 3)
            main(6, 0, 6)
            main(7, 1, 7)
            divide(7, 0)
            divide(7, 1)
            read_s(7)


def moe(nc, io, S):
    E = EXPERTS
    UNITS = CHUNKS * (E + 1)
    with ExitStack() as ctx:
        def sb(name, shape, dt=F32):
            return ctx.enter_context(nc.sbuf_tensor("m_" + name, shape, dt))

        def sem(name):
            return ctx.enter_context(nc.semaphore("m_" + name))

        wg = sb("wg", [C, E + 1, DFF])
        wu = sb("wu", [C, E + 1, DFF])
        wd = sb("wd", [P, E + 1, CHUNKS, C])
        xs = [sb(f"xs{i}", [C, T]) for i in range(2)]
        xt = [sb(f"xt{i}", [P, TT, C]) for i in range(2)]
        st = [sb(f"st{i}", [P, TT, C]) for i in range(2)]
        wt = [sb(f"wt{i}", [P, TT, E]) for i in range(2)]
        acc = [sb(f"acc{i}", [P, TT, C]) for i in range(2)]
        weighed = sb("weighed", [P, TT, C])
        act_g = [sb(f"act{i}", [P, T]) for i in range(2)]
        hid = [sb(f"hid{i}", [P, T]) for i in range(2)]
        gated = sb("gated", [P, TT, C])
        prod = sb("prod", [P, TT, C])
        xo = [sb(f"xo{i}", [P, TT, C]) for i in range(2)]
        GROUPS = ((0, 1), (1, 3), (3, 5), (5, E + 1))
        weights_in = [sem(f"weights_in{i}") for i in range(len(GROUPS))]
        inputs_in = sem("inputs_in")
        weighed_done, acc_done = sem("weighed_done"), sem("acc_done")
        g_mm, u_mm, d_mm = sem("g_mm"), sem("u_mm"), sem("d_mm")
        silu_done, h_done = sem("silu_done"), sem("h_done")
        out_mm, out_silu, prod_done, x_done, x_out = (sem("out_mm"), sem("out_silu"), sem("prod_done"), sem("x_done"),
                                                      sem("x_out"))
        gate_bank, up_bank = S["bank"], S["quad"]

        def out_bank(par, e):
            return S["quad"][:, 2 + (par + e) % 2, :]

        block = ctx.enter_context(nc.Block())

        @block.sync
        def _(sp):
            def known(value):
                return value if isinstance(value, int) else sp.snap(sp.to_reg(value))

            def load(b, par):
                tile0, col = known(b * TT), known(b * T)
                before, weighed_all, finished, used = known(64 * b), known(E * (b - 1)), known(b - 1), known(UNITS * (b - 1))
                wait(sp, inputs_in, before)
                wait(sp, weighed_done, weighed_all)
                wait(sp, u_mm, used)
                wait(sp, x_done, finished)
                sp.dma_start(xs[par][:, :], S["xnT"][:, bass.ds(col, T)]).then_inc(inputs_in, 16)
                sp.dma_start(wt[par][:, :, :], S["route"][:, bass.ds(tile0, TT), :]).then_inc(inputs_in, 16)
                sp.dma_start(xt[par][:, :, :], S["x"][:, bass.ds(tile0, TT), :]).then_inc(inputs_in, 16)
                sp.dma_start(st[par][:, :, :], S["s"][:, bass.ds(tile0, TT), :]).then_inc(inputs_in, 16)

            def store(b, par):
                tile0, before, done = known(b * TT), known(16 * b), known(b + 1)
                wait(sp, x_out, before)
                wait(sp, x_done, done)
                sp.dma_start(S["x"][:, bass.ds(tile0, TT), :], xo[par][:, :, :]).then_inc(x_out, 16)

            sp.dma_start(wg[:, 0, :], io["L0_ffn_ws_gate"]).then_inc(weights_in[0], 16)
            load(0, 0)
            sp.dma_start(wu[:, 0, :], io["L0_ffn_ws_up"]).then_inc(weights_in[0], 16)
            sp.dma_start(wd[:, 0, :, :], io["L0_ffn_ws_down"].rearrange("(k p) o -> p k o", p=P)).then_inc(weights_in[0], 16)
            for (a, z), arrived in zip(GROUPS[1:], weights_in[1:]):
                e = slice(a - 1, z - 1)
                sp.dma_start(wg[:, a:z, :], io["L0_ffn_w_gate"][e].rearrange("e c d -> c e d")).then_inc(arrived, 16)
                sp.dma_start(wu[:, a:z, :], io["L0_ffn_w_up"][e].rearrange("e c d -> c e d")).then_inc(arrived, 16)
                for k in range(CHUNKS):
                    sp.dma_start(wd[:, a:z, k, :], io["L0_ffn_w_down"][e, k * P:(k + 1) * P, :].rearrange("e p o -> p e o"))\
                      .then_inc(arrived, 16)
            load(1, 1)
            with sp.Fori(0, B // 2 - 1) as j:
                for par in range(2):
                    store(j * 2 + par, par)
                    load(j * 2 + par + 2, par)
            store(B - 2, 0)
            store(B - 1, 1)
            sp.wait_ge(x_out, 16 * B)

        @block.tensor
        def _(pe):
            def gate_up(b, par, u):
                e, k = u // CHUNKS, u % CHUNKS
                cols = slice(k * P, (k + 1) * P)
                wait(pe, silu_done, UNITS * b + u - 1)
                pe.matmul(gate_bank[u % 2][:, :], wg[:, e, cols], xs[par][:, :], start=True, stop=True).then_inc(g_mm, 1)
                wait(pe, h_done, UNITS * b + u - 1)
                pe.matmul(up_bank[:, u % 2, :], wu[:, e, cols], xs[par][:, :], start=True, stop=True).then_inc(u_mm, 1)

            def down(b, par, u):
                e, k = u // CHUNKS, u % CHUNKS
                wait(pe, h_done, UNITS * b + u + 1)
                if k == 0:
                    wait(pe, acc_done, (E + 1) * b + e - 1)
                for t in range(TT):
                    last = pe.matmul(out_bank(par, e)[:, t * P:(t + 1) * P], hid[u % 2][:, t * P:(t + 1) * P], wd[:, e, k, :],
                                     start=(k == 0 and t == 0), stop=(k == CHUNKS - 1), skip_group_check=True)
                last.then_inc(d_mm, 1)

            def sequence(b, par, first=False):
                wait(pe, inputs_in, 64 * (b + 1))
                for u in range(UNITS):
                    for (a, z), arrived in zip(GROUPS[1:], weights_in[1:]):
                        if first and u == CHUNKS * a:
                            pe.wait_ge(arrived, 16 * 4)
                    gate_up(b, par, u)
                    if u >= 1:
                        down(b, par, u - 1)
                    elif not first:
                        down(b - 1, 1 - par, UNITS - 1)

            pe.wait_ge(weights_in[0], 48)
            sequence(0, 0, True)
            sequence(1, 1)
            with pe.Fori(1, B // 2) as j:
                for par in range(2):
                    sequence(j * 2 + par, par)
            down(B - 1, 1, UNITS - 1)

        @block.scalar
        def _(act):
            def finish(b, par):
                wait(act, acc_done, (E + 1) * (b + 1))
                wait(act, prod_done, b)
                act.activation(gated[:, :, :], acc[par][:, :, :], ACT.Silu).then_inc(out_silu, 1)

            def sequence(b, par, first=False):
                for u in range(UNITS):
                    if u == 4 and not first:
                        finish(b - 1, 1 - par)
                    wait(act, g_mm, UNITS * b + u + 1)
                    wait(act, h_done, UNITS * b + u - 1)
                    act.activation(act_g[u % 2][:, :], gate_bank[u % 2][:, :], ACT.Silu).then_inc(silu_done, 1)

            sequence(0, 0, True)
            sequence(1, 1)
            with act.Fori(1, B // 2) as j:
                for par in range(2):
                    sequence(j * 2 + par, par)
            finish(B - 1, 1)

        @block.vector
        def _(dve):
            def accumulate(b, par, e):
                wait(dve, d_mm, UNITS * b + CHUNKS * (e + 1))
                out = out_bank(par, e).rearrange("p (t c) -> p t c", t=TT)
                if e == 0:
                    wait(dve, out_silu, b - 1)
                    dve.tensor_copy(acc[par][:, :, :], out).then_inc(acc_done, 1)
                else:
                    wait(dve, acc_done, (E + 1) * b + e)
                    dve.tensor_tensor(weighed[:, :, :], out, wt[par][:, :, e - 1:e].broadcast_to([P, TT, C]),
                                      ALU.mult).then_inc(weighed_done, 1)
                    wait(dve, weighed_done, E * b + e)
                    dve.tensor_tensor(acc[par][:, :, :], acc[par][:, :, :], weighed[:, :, :], ALU.add).then_inc(acc_done, 1)

            def finish(b, par):
                wait(dve, out_silu, b + 1)
                dve.tensor_tensor(prod[:, :, :], gated[:, :, :], st[par][:, :, :], ALU.mult).then_inc(prod_done, 1)
                wait(dve, prod_done, b + 1)
                wait(dve, x_out, 16 * (b - 1))
                dve.tensor_tensor(xo[par][:, :, :], prod[:, :, :], xt[par][:, :, :], ALU.add).then_inc(x_done, 1)

            def sequence(b, par, first=False):
                wait(dve, inputs_in, 64 * (b + 1))
                for u in range(UNITS):
                    wait(dve, silu_done, UNITS * b + u + 1)
                    wait(dve, u_mm, UNITS * b + u + 1)
                    wait(dve, d_mm, UNITS * b + u - 1)
                    dve.tensor_tensor(hid[u % 2][:, :], act_g[u % 2][:, :], up_bank[:, u % 2, :], ALU.mult).then_inc(h_done, 1)
                    if u == 1 and not first:
                        accumulate(b - 1, 1 - par, E)
                    if u % 2 and u >= 3:
                        accumulate(b, par, (u - 3) // 2)
                    if u == 6 and not first:
                        finish(b - 1, 1 - par)

            sequence(0, 0, True)
            sequence(1, 1)
            with dve.Fori(1, B // 2) as j:
                for par in range(2):
                    sequence(j * 2 + par, par)
            accumulate(B - 1, 1, E)
            finish(B - 1, 1)


def coupling(nc, io, S):
    CYCLES = 3
    D2, D3 = C // 2, C // 4
    with ExitStack() as ctx:
        def sb(name, shape, dt=F32):
            return ctx.enter_context(nc.sbuf_tensor("c_" + name, shape, dt))

        def sem(name):
            return ctx.enter_context(nc.semaphore("c_" + name))

        out = sb("out", [C, B * T])
        w1, w2, w3, w4 = sb("w1", [C, C]), sb("w2", [C, D2]), sb("w3", [P, D3]), sb("w4", [P, 1])
        v1, v2, v3 = sb("v1", [C, D2]), sb("v2", [P, D3]), sb("v3", [P, 1])
        bias = sb("bias", [P, 8])
        half = sb("half", [P, 4])
        h1 = [sb(f"h1_{i}", [P, T]) for i in range(2)]
        h2, h3 = sb("h2", [P, T]), sb("h3", [P, T])
        tf = sb("tf", [P, T])
        coup = sb("coup", [P, T])
        delta = sb("delta", [P, T])
        means = sb("means", [C, B])
        context = sb("context", [C, B])
        g1, g2, gt, base = sb("g1", [P, B]), sb("g2", [P, B]), sb("gt", [P, B]), sb("base", [P, B])
        gate = [sb(f"gate{i}", [C, T]) for i in range(2)]
        loaded, copied, zeroed = sem("loaded"), sem("copied"), sem("zeroed")
        prepared = sem("prepared")
        g_mm, g_act, g_vec = sem("g_mm"), sem("g_act"), sem("g_vec")
        mm = [sem(f"mm{i}") for i in range(4)]
        lay = [sem(f"layer{i}") for i in range(4)]
        twisted = sem("twisted")
        coupled, delta_done, updated = sem("coupled"), sem("delta_done"), sem("updated")
        gated, turned, stored = sem("gated"), sem("turned"), sem("stored")
        bank, quad, misc = S["bank"], S["quad"], S["misc"]
        block = ctx.enter_context(nc.Block())
        B1, B2, B3, B4, G1, G2, G3, AR = range(8)

        def cols(t):
            return slice(T * t, T * (t + 1))

        @block.sync
        def _(sp):
            n = 0
            for dst, name, rows in ((w1, "cn_w1", C), (w2, "cn_w2", C), (w3, "cn_w3", D2), (w4, "cn_w4", D3),
                                    (v1, "gc_w1", C), (v2, "gc_w2", D2), (v3, "gc_w3", D3)):
                if rows < C:
                    sp.wait_ge(zeroed, 1)
                sp.dma_start(dst[0:rows, :], io["L1_ffn_" + name]).then_inc(loaded, 16)
            for k, name, rows in ((B1, "cn_b1", C), (B2, "cn_b2", D2), (B3, "cn_b3", D3), (G1, "gc_b1", D2), (G2, "gc_b2", D3)):
                sp.dma_start(bias[0:rows, k:k + 1], io["L1_ffn_" + name].rearrange("(c o) -> c o", o=1)).then_inc(loaded, 16)
            for k, name in ((B4, "cn_b4"), (G3, "gc_b3"), (AR, "adaptive_range")):
                sp.dma_start(bias[:, k:k + 1], io["L1_ffn_" + name].rearrange("(o c) -> o c", o=1).broadcast_to([P, 1]))\
                  .then_inc(loaded, 16)

        LOADED = 16 * 15

        @block.gpsimd
        def _(pool):
            for n, a in enumerate((w3, w4, v2, v3, bias, g1, g2)):
                last = pool.memset(a[:, :], 0.0)
            last.then_inc(zeroed, 1)
            pool.memset(h2[:, :], 0.0)
            pool.memset(h3[:, :], 0.0).then_inc(prepared, 1)
            for t in range(B):
                pool.tensor_copy(out[:, cols(t)], S["xnT"][:, cols(t)]).then_inc(copied, 1)

        def item(n):
            return n % B

        @block.tensor
        def _(pe):
            pe.wait_ge(loaded, LOADED)
            pe.wait_ge(g_vec, 2)
            pe.matmul(misc[0:D2, 0:B], v1[:, :], context[:, :], start=True, stop=True).then_inc(g_mm, 1)
            pe.wait_ge(g_act, 1)
            pe.matmul(misc[0:D3, 16:16 + B], v2[:, :], g1[:, :], start=True, stop=True).then_inc(g_mm, 1)
            pe.wait_ge(g_act, 2)
            pe.matmul(misc[:, 32:32 + B], v3[:, 0:1].broadcast_to([P, P]), g2[:, :], start=True, stop=True).then_inc(g_mm, 1)
            pe.wait_ge(prepared, 1)

            def layer(s, n, t):
                if s == 0:
                    wait(pe, updated, n - B + 1)
                    if isinstance(n, int) and n < B:
                        wait(pe, copied, n + 1)
                    wait(pe, lay[0], n - 1)
                    pe.matmul(bank[t % 2][:, :], w1[:, :], out[:, cols(t)], start=True, stop=True).then_inc(mm[0], 1)
                elif s == 1:
                    wait(pe, lay[0], n + 1)
                    wait(pe, lay[1], n)
                    pe.matmul(quad[0:D2, 0, :], w2[:, :], h1[t % 2][:, :], start=True, stop=True).then_inc(mm[1], 1)
                elif s == 2:
                    wait(pe, lay[1], n + 1)
                    wait(pe, lay[2], n)
                    pe.matmul(quad[0:D3, 1, :], w3[:, :], h2[:, :], start=True, stop=True).then_inc(mm[2], 1)
                else:
                    wait(pe, lay[2], n + 1)
                    wait(pe, lay[3], n)
                    pe.matmul(quad[:, 2, :], w4[:, 0:1].broadcast_to([P, P]), h3[:, :], start=True, stop=True).then_inc(mm[3], 1)
                    wait(pe, delta_done, n)
                    pe.matmul(quad[:, 3, :], S["twist"], out[:, cols(t)], start=True, stop=True).then_inc(twisted, 1)

            def cycle(c, first):
                for k in range(B):
                    for s in range(4):
                        if not (first and k < s):
                            layer(s, c * B + k - s, item(k - s))

            cycle(0, True)
            with pe.Fori(1, CYCLES) as c:
                cycle(c, False)
            for k in range(3):
                for s in range(k + 1, 4):
                    layer(s, CYCLES * B + k - s, item(k - s))
            for t in range(B):
                pe.wait_ge(gated, t + 1)
                wait(pe, stored, t - 1)
                for m in range(TT):
                    last = pe.transpose(bank[t % 2][:, m * P:(m + 1) * P], gate[t % 2][:, m * P:(m + 1) * P], S["ident"])
                last.then_inc(turned, 1)

        @block.scalar
        def _(act):
            act.wait_ge(g_mm, 1)
            act.activation(g1[0:D2, :], misc[0:D2, 0:B], ACT.Gelu, bias=bias[0:D2, G1:G1 + 1]).then_inc(g_act, 1)
            act.wait_ge(g_mm, 2)
            act.activation(g2[0:D3, :], misc[0:D3, 16:16 + B], ACT.Gelu, bias=bias[0:D3, G2:G2 + 1]).then_inc(g_act, 1)
            act.wait_ge(g_mm, 3)
            act.wait_ge(g_vec, 3)
            act.activation(gt[:, :], misc[:, 32:32 + B], ACT.Tanh, bias=half[:, 1:2], scale=0.5).then_inc(g_act, 1)
            act.wait_ge(prepared, 1)

            def layer(s, n, t):
                wait(act, mm[s], n + 1)
                if s == 0:
                    wait(act, mm[1], n - 1)
                    act.activation(h1[t % 2][:, :], bank[t % 2][:, :], ACT.Gelu, bias=bias[:, B1:B1 + 1]).then_inc(lay[0], 1)
                elif s == 1:
                    wait(act, mm[2], n)
                    act.activation(h2[0:D2, :], quad[0:D2, 0, :], ACT.Gelu, bias=bias[0:D2, B2:B2 + 1]).then_inc(lay[1], 1)
                elif s == 2:
                    wait(act, mm[3], n)
                    act.activation(h3[0:D3, :], quad[0:D3, 1, :], ACT.Gelu, bias=bias[0:D3, B3:B3 + 1]).then_inc(lay[2], 1)
                else:
                    wait(act, coupled, n)
                    act.activation(tf[:, :], quad[:, 2, :], ACT.Tanh, bias=half[:, 0:1], scale=0.5).then_inc(lay[3], 1)

            def cycle(c, first):
                for k in range(B):
                    for s in range(4):
                        if not (first and k < s):
                            layer(s, c * B + k - s, item(k - s))

            cycle(0, True)
            with act.Fori(1, CYCLES) as c:
                cycle(c, False)
            for k in range(3):
                for s in range(k + 1, 4):
                    layer(s, CYCLES * B + k - s, item(k - s))
            for t in range(B):
                act.wait_ge(updated, (CYCLES - 1) * B + t + 1)
                wait(act, turned, t - 1)
                act.activation(gate[t % 2][:, :], out[:, cols(t)], ACT.Silu).then_inc(gated, 1)

        @block.vector
        def _(dve):
            for t in range(B):
                last = dve.tensor_reduce(means[:, t:t + 1], S["xnT"][:, cols(t)], AX_X, ALU.add)
            last.then_inc(g_vec, 1)
            dve.wait_ge(g_vec, 1)
            dve.tensor_scalar(context[:, :], means[:, :], 1.0 / T, None, ALU.mult).then_inc(g_vec, 1)
            dve.wait_ge(loaded, LOADED)
            dve.tensor_scalar(half[:, 0:1], bias[:, B4:B4 + 1], 0.5, None, ALU.mult)
            dve.tensor_scalar(half[:, 1:2], bias[:, G3:G3 + 1], 0.5, None, ALU.mult)
            dve.tensor_scalar(half[:, 2:3], bias[:, AR:AR + 1], 0.3, None, ALU.mult)
            dve.tensor_scalar(half[:, 3:4], bias[:, AR:AR + 1], 0.7, None, ALU.mult).then_inc(g_vec, 1)
            dve.wait_ge(g_vec, 3)
            dve.wait_ge(g_act, 3)
            dve.tensor_scalar(base[:, :], gt[:, :], half[:, 3:4], 0.1, ALU.mult, ALU.add).then_inc(g_vec, 1)
            dve.wait_ge(g_vec, 4)

            def update(n, t):
                wait(dve, lay[3], n + 1)
                wait(dve, delta_done, n)
                dve.tensor_scalar(coup[:, :], tf[:, :], half[:, 2:3], base[:, t:t + 1], ALU.mult, ALU.add).then_inc(coupled, 1)
                wait(dve, coupled, n + 1)
                wait(dve, twisted, n + 1)
                wait(dve, updated, n)
                dve.tensor_tensor(delta[:, :], coup[:, :], quad[:, 3, :], ALU.mult).then_inc(delta_done, 1)
                wait(dve, delta_done, n + 1)
                dve.tensor_tensor(out[:, cols(t)], out[:, cols(t)], delta[:, :], ALU.add).then_inc(updated, 1)

            for t in range(B):
                update(t, t)
            with dve.Fori(1, CYCLES) as c:
                for t in range(B):
                    update(c * B + t, t)
            for t in range(B):
                dve.wait_ge(turned, t + 1)
                dve.tensor_copy(S["s"][:, TT * t:TT * (t + 1), :], bank[t % 2][:, :].rearrange("p (m c) -> p m c", m=TT))\
                   .then_inc(stored, 1)


def attention1(nc, io, S):
    with ExitStack() as ctx:
        def sb(name, shape, dt=F32):
            return ctx.enter_context(nc.sbuf_tensor("a1_" + name, shape, dt))

        def sem(name):
            return ctx.enter_context(nc.semaphore("a1_" + name))

        xs = [sb(f"xs{i}", [C, T]) for i in range(2)]
        full = [sb(f"full{i}", [P, T]) for i in range(2)]
        rest = sb("rest", [P, T])
        parts = [sb(f"parts{i}", [P, 3, T], BF16) for i in range(4)]
        qs, ks = [q[0:KROWS] for q in S["qs"]], [k[0:KROWS] for k in S["ks"]]
        va = [sb(f"va{i}", [P, TT, H, STRIP]) for i in range(2)]
        vext = [sb(f"vext{i}", [P, TT, NCOMP]) for i in range(2)]
        probs = sb("probs", [P, 8, T])
        osb = [sb(f"osb{i}", [P, NG, T]) for i in range(2)]
        den = sb("den", [P, 2, H])
        rden = sb("rden", [P, 2, H])
        yn = sb("yn", [P, TT, C])
        yT = S["wT"]
        xg = sb("xg", [P, 2, TT, C])
        prod = yn
        so = sb("so", [P, TT, C])

        zeroed, filled = sem("zeroed"), sem("filled")
        xs_in, xg_in = sem("xs_in"), sem("xg_in")
        qk_mm, qk_read, qk_cast = sem("qk_mm"), sem("qk_read"), sem("qk_cast")
        rested, second, split = sem("rested"), sem("second"), sem("split")
        stack_a, stack_b = sem("stack_a"), sem("stack_b")
        v_mm, v_read = sem("v_mm"), sem("v_read")
        s_mm, squared, masked = sem("s_mm"), sem("squared"), sem("masked")
        av_mm, o_read = sem("av_mm"), sem("o_read")
        c_mm, floored, rec, yn_done = sem("c_mm"), sem("floored"), sem("rec"), sem("yn_done")
        yt_mm, yt_read = sem("yt_mm"), sem("yt_read")
        pr_mm, prod_done, so_done, so_out = sem("pr_mm"), sem("prod_done"), sem("so_done"), sem("so_out")
        quad, av, misc = S["quad"], S["av"], S["bank"][0]
        misc2 = S["bank"][1]
        block = ctx.enter_context(nc.Block())
        STACK = 16 * 2 * len(PAIRS)


        @block.sync
        def _(sp):
            def known(value):
                return value if isinstance(value, int) else sp.snap(sp.to_reg(value))

            def load_xs(b, par):
                col, mine, used, projected = known(b * T), known(16 * b), known(b - 1), known(4 * (b - 1))
                wait(sp, xs_in, mine)
                wait(sp, qk_mm, projected)
                wait(sp, v_mm, used)
                sp.dma_start(xs[par][:, :], S["xnT"][:, bass.ds(col, T)]).then_inc(xs_in, 16)

            def load_xg(b):
                tile0, mine, used = known(b * TT), known(32 * b), known(b)
                wait(sp, xg_in, mine)
                wait(sp, so_done, used)
                sp.dma_start(xg[:, 0], S["x"][:, bass.ds(tile0, TT), :]).then_inc(xg_in, 16)
                sp.dma_start(xg[:, 1], S["s"][:, bass.ds(tile0, TT), :]).then_inc(xg_in, 16)

            def stack(b, par, half):
                done = stack_b if half else stack_a
                split_now, scores_now, before = known(4 * b + 2 + 2 * half), known(64 * (b - 2) + 32 * (half + 1)), known(STACK * b)
                wait(sp, done, before)
                wait(sp, split, split_now)
                wait(sp, s_mm, scores_now)
                heads = slice(8 * half, 8 * half + 8)
                for n, (i, j) in enumerate(PAIRS):
                    for op, (dst, part) in enumerate(((qs, i), (ks, j))):
                        sp.dma_start(dst[par][DQ1 * n:DQ1 * (n + 1), heads, :], parts[2 * half + op][:, part, :]).then_inc(done, 16)

            def store(b):
                row, summed, before = known(b), known(b + 1), known(16 * b)
                wait(sp, so_out, before)
                wait(sp, so_done, summed)
                sp.dma_start(io["out"].rearrange("b (t p) c -> p b t c", p=P)[:, bass.ds(row, 1), :, :],
                             so[:, :, :]).then_inc(so_out, 16)

            def main(i, par, n):
                if n <= 5:
                    stack(i + 2, par, 0)
                if n >= 1:
                    store(i - 1)
                    load_xg(i)
                if n <= 4:
                    load_xs(i + 3, 1 - par)
                if n <= 5:
                    stack(i + 2, par, 1)

            load_xs(0, 0)
            load_xs(1, 1)
            load_xg(0)
            stack(0, 0, 0)
            stack(0, 0, 1)
            load_xs(2, 0)
            stack(1, 1, 0)
            stack(1, 1, 1)
            main(0, 0, 0)
            main(1, 1, 1)
            with sp.Fori(1, B // 2 - 2) as j:
                main(j * 2, 0, 2)
                main(j * 2 + 1, 1, 3)
            main(B - 4, 0, 4)
            main(B - 3, 1, 5)
            main(B - 2, 0, 6)
            main(B - 1, 1, 7)
            store(B - 1)
            sp.wait_ge(so_out, 16 * B)

        @block.gpsimd
        def _(pool):
            def split_one(c, k):
                f, r, pt = full[k % 2], rest, parts[k]
                wait(pool, qk_cast, c + 1)
                wait(pool, split, c)
                pool.tensor_tensor(r[:, :], f[:, :], pt[:, 0, :], ALU.subtract).then_inc(rested, 1)
                pool.tensor_tensor(pt[:, 1, :], f[:, :], pt[:, 0, :], ALU.subtract).then_inc(second, 1)
                wait(pool, rested, c + 1)
                wait(pool, second, c + 1)
                pool.tensor_tensor(pt[:, 2, :], r[:, :], pt[:, 1, :], ALU.subtract).then_inc(split, 1)

            for b in range(4):
                for k in range(4):
                    split_one(4 * b + k, k)
            with pool.Fori(1, B // 2 - 1) as j:
                for n in range(2):
                    for k in range(4):
                        split_one(8 * j + (4 * (n + 2) + k), k)

        @block.tensor
        def _(pe):
            def q_k(b, par, k):
                half, op = k // 2, k % 2
                if k == 0:
                    wait(pe, xs_in, 16 * (b + 1))
                w = S["wk1T"] if op else S["wq1T"]
                wait(pe, qk_read, 4 * b + k)
                pe.matmul(misc2[:, :], w[:, half * P:(half + 1) * P], xs[par][:, :], start=True, stop=True).then_inc(qk_mm, 1)

            def values(b, par):
                for t in range(TT):
                    last = pe.matmul(misc[:, t * P:(t + 1) * P], xs[par][:, t * P:(t + 1) * P], S["wv1T"],
                                     start=True, stop=True)
                last.then_inc(v_mm, 1)

            def score(b, par, t, j):
                g, kt = t // TT, t % TT
                h, n = GH * g + j, 4 * t + j
                if t == 0 and j == 0:
                    wait(pe, stack_a, STACK * (b + 1))
                if t == 8 and j == 0:
                    wait(pe, stack_b, STACK * (b + 1))
                wait(pe, squared, 64 * b + n - 3)
                pe.matmul(quad[:, n % 4, kt * P:T], ks[par][:, h, kt * P:(kt + 1) * P], qs[par][:, h, kt * P:T],
                          start=True, stop=True).then_inc(s_mm, 1)

            def weigh(b, par, t):
                g, kt = t // TT, t % TT
                wait(pe, masked, 64 * b + 4 * t + 4)
                if kt == 0:
                    wait(pe, o_read, 4 * b + g)
                if t == 0:
                    wait(pe, v_read, 2 * b + 2)
                for j in range(GH):
                    last = pe.matmul(av[STRIP * j:STRIP * (j + 1), kt * P:T], va[par][:, kt, GH * g + j, :],
                                     probs[:, (4 * t + j) % 8, kt * P:T], start=(kt == 0), stop=(kt == TT - 1))
                last.then_inc(av_mm, 1)

            def gather(b, par, pair):
                if pair == 0:
                    wait(pe, o_read, 4 * b + 4)
                for k in range(2):
                    t = 2 * pair + k
                    for kt in range(t + 1):
                        pe.matmul(misc[:, k * NCOMP:(k + 1) * NCOMP], S["tri"] if kt == t else S["ones"], vext[par][:, kt, :],
                                  start=(kt == 0), stop=False)
                    for g in range(NG):
                        last = pe.matmul(misc[:, k * NCOMP:(k + 1) * NCOMP], osb[par][:, g, t * P:(t + 1) * P],
                                         S["sel"][:, g * NCOMP:(g + 1) * NCOMP], start=False, stop=(g == NG - 1))
                last.then_inc(c_mm, 1)

            def finish_step(i, par, k):
                if k == 0:
                    gather(i, par, 0)
                elif k == 1:
                    wait(pe, yn_done, 2 * i + 1)
                    gather(i, par, 1)
                elif k == 2:
                    wait(pe, yn_done, 2 * i + 2)
                    for t in range(TT):
                        last = pe.transpose(misc[:, t * P:(t + 1) * P], yn[:, t, :], S["ident"])
                    last.then_inc(yt_mm, 1)
                else:
                    wait(pe, yt_read, i + 1)
                    for t in range(TT):
                        last = pe.matmul(misc[:, t * P:(t + 1) * P], yT[:, t * P:(t + 1) * P], S["wo1T"],
                                         start=True, stop=True)
                    last.then_inc(pr_mm, 1)

            def main(i, par, n):
                for t in range(STEPS):
                    for j in range(GH):
                        score(i, par, t, j)
                    if t >= 1:
                        weigh(i, par, t - 1)
                    elif n >= 1:
                        weigh(i - 1, 1 - par, STEPS - 1)
                    if n <= 5 and t in (1, 2, 11, 12):
                        q_k(i + 2, par, t - 1 if t < 8 else t - 9)
                    if 3 <= t <= 6 and n >= 1:
                        if t == 3:
                            wait(pe, v_read, 2 * i + 2)
                        finish_step(i - 1, 1 - par, t - 3)
                    if t == 7 and n <= 6:
                        wait(pe, prod_done, i) if n >= 1 else wait(pe, v_read, 2 * i + 2)
                        values(i + 1, 1 - par)

            for b in range(2):
                for k in range(4):
                    q_k(b, b, k)
                if b == 0:
                    values(0, 0)
            main(0, 0, 0)
            main(1, 1, 1)
            with pe.Fori(1, B // 2 - 1) as j:
                main(j * 2, 0, 2)
                main(j * 2 + 1, 1, 3)
            main(B - 2, 0, 6)
            main(B - 1, 1, 7)
            weigh(B - 1, 1, STEPS - 1)
            for k in range(4):
                if k == 0:
                    pe.wait_ge(prod_done, B - 1)
                finish_step(B - 1, 1, k)

        @block.scalar
        def _(act):
            def read_qk(b, k):
                half, op = k // 2, k % 2
                wait(act, qk_mm, 4 * b + k + 1)
                wait(act, split, 4 * b + k - 1)
                act.activation(full[op][:, :], misc2[:, :], ACT.Copy).then_inc(qk_read, 1)

            def squares(b, t):
                kt = t % TT
                for j in range(GH):
                    n = 4 * t + j
                    if j == 0:
                        wait(act, av_mm, 16 * b + t - 1)
                    wait(act, s_mm, 64 * b + n + 1)
                    act.activation(probs[:, n % 8, kt * P:T], quad[:, n % 4, kt * P:T], ACT.Square, bias=1.0, scale=0.25)\
                       .then_inc(squared, 1)

            def read_o(b, par, g):
                wait(act, av_mm, 16 * b + 4 * g + 4)
                wait(act, c_mm, 2 * (b - 1))
                act.activation(osb[par][:, g, :], av[:, :], ACT.Copy).then_inc(o_read, 1)

            def read_yT(b):
                wait(act, yt_mm, b + 1)
                wait(act, pr_mm, b)
                act.activation(yT[:, :], misc[:, :], ACT.Copy).then_inc(yt_read, 1)

            def main(i, par, n):
                for t in range(STEPS):
                    squares(i, t)
                    if t == 0 and n >= 1:
                        read_o(i - 1, 1 - par, NG - 1)
                    if t > 0 and t % TT == 0:
                        read_o(i, par, t // TT - 1)
                    if n <= 5 and t in (1, 2, 11, 12):
                        read_qk(i + 2, t - 1 if t < 8 else t - 9)
                    if t == 5 and n >= 1:
                        read_yT(i - 1)

            for b in range(2):
                for k in range(4):
                    read_qk(b, k)
            main(0, 0, 0)
            main(1, 1, 1)
            with act.Fori(1, B // 2 - 1) as j:
                main(j * 2, 0, 2)
                main(j * 2 + 1, 1, 3)
            main(B - 2, 0, 6)
            main(B - 1, 1, 7)
            read_o(B - 1, 1, NG - 1)
            read_yT(B - 1)

        @block.vector
        def _(dve):
            for i in range(2):
                dve.memset(va[i][:, :, :, :].bitcast(U32), 0).then_inc(zeroed, 1)
            for i in range(2):
                dve.memset(vext[i][:, :, C:NCOMP], 1.0)
            dve.wait_ge(zeroed, 2)
            for i in range(2):
                dve.memset(va[i][:, :, :, DH:DH + 1], 1.0).then_inc(filled, 1)
            dve.wait_ge(filled, 2)

            def cast(b, k):
                half, op = k // 2, k % 2
                wait(dve, qk_read, 4 * b + k + 1)
                wait(dve, stack_b if half else stack_a, STACK * b)
                dve.tensor_copy(parts[k][:, 0, :], full[op][:, :]).then_inc(qk_cast, 1)

            def mask(b, t):
                kt = t % TT
                for j in range(GH):
                    n = 4 * t + j
                    block_ = probs[:, n % 8, kt * P:(kt + 1) * P]
                    wait(dve, squared, 64 * b + n + 1)
                    dve.tensor_tensor(block_, block_, S["tri"], ALU.mult).then_inc(masked, 1)

            def read_v(b, par):
                wait(dve, v_mm, b + 1)
                wait(dve, av_mm, 16 * (b - 1))
                wait(dve, c_mm, 2 * (b - 1))
                dve.tensor_copy(va[par][:, :, :, 0:DH], misc[:, :].rearrange("p (t h d) -> p t h d", t=TT, d=DH)).then_inc(v_read, 1)
                dve.tensor_copy(vext[par][:, :, 0:C], misc[:, :].rearrange("p (t c) -> p t c", t=TT)).then_inc(v_read, 1)

            def divide(b, pair):
                c = 2 * b + pair + 1
                wait(dve, c_mm, c)
                m = misc[:, 0:2 * NCOMP].rearrange("p (k n) -> p k n", k=2)
                dve.tensor_scalar(den[:, :, :], m[:, :, C:NCOMP], 2 * EPS_L1, None, ALU.add).then_inc(floored, 1)
                wait(dve, floored, c)
                dve.reciprocal(rden[:, :, :], den[:, :, :]).then_inc(rec, 1)
                wait(dve, rec, c)
                if pair == 0:
                    wait(dve, so_done, b)
                dve.tensor_tensor(yn[:, 2 * pair:2 * pair + 2, :].rearrange("p k (h d) -> p k h d", d=DH),
                                  m[:, :, 0:C].rearrange("p k (h d) -> p k h d", d=DH),
                                  rden[:, :, :, None].broadcast_to([P, 2, H, DH]), ALU.mult).then_inc(yn_done, 1)

            def result(b):
                wait(dve, pr_mm, b + 1)
                wait(dve, xg_in, 32 * (b + 1))
                dve.tensor_tensor(prod[:, :, :], misc[:, :].rearrange("p (t c) -> p t c", t=TT), xg[:, 1], ALU.mult).then_inc(prod_done, 1)
                wait(dve, prod_done, b + 1)
                wait(dve, so_out, 16 * b)
                dve.tensor_tensor(so[:, :, :], prod[:, :, :], xg[:, 0], ALU.add).then_inc(so_done, 1)

            def main(i, par, n):
                for t in range(STEPS):
                    mask(i, t)
                    if n <= 5 and t in (1, 2, 11, 12):
                        cast(i + 2, t - 1 if t < 8 else t - 9)
                    if t in (3, 4) and n >= 1:
                        divide(i - 1, t - 3)
                    if t == 6 and n >= 1:
                        result(i - 1)
                    if t == 7 and n <= 6:
                        read_v(i + 1, 1 - par)

            for b in range(2):
                for k in range(4):
                    cast(b, k)
            read_v(0, 0)
            main(0, 0, 0)
            main(1, 1, 1)
            with dve.Fori(1, B // 2 - 1) as j:
                main(j * 2, 0, 2)
                main(j * 2 + 1, 1, 3)
            main(B - 2, 0, 6)
            main(B - 1, 1, 7)
            divide(B - 1, 0)
            divide(B - 1, 1)
            result(B - 1)


_INS = ["L0_attn_x", "L0_attn_Wq", "L0_attn_bq", "L0_attn_Wk", "L0_attn_bk", "L0_attn_Wv", "L0_attn_bv", "L0_attn_Wp",
        "L0_attn_bp", "L0_ffn_gate_w", "L0_ffn_w_gate", "L0_ffn_w_up", "L0_ffn_w_down", "L0_ffn_ws_gate",
        "L0_ffn_ws_up", "L0_ffn_ws_down", "L1_attn_Wq", "L1_attn_Wk", "L1_attn_Wv", "L1_attn_Wo", "L1_ffn_cn_w1",
        "L1_ffn_cn_b1", "L1_ffn_cn_w2", "L1_ffn_cn_b2", "L1_ffn_cn_w3", "L1_ffn_cn_b3", "L1_ffn_cn_w4",
        "L1_ffn_cn_b4", "L1_ffn_gc_w1", "L1_ffn_gc_b1", "L1_ffn_gc_w2", "L1_ffn_gc_b2", "L1_ffn_gc_w3",
        "L1_ffn_gc_b3", "L1_ffn_adaptive_range"]


def kernel(**inputs):
    import concourse.bacc as bacc
    from concourse.bass_utils import run_bass_kernel_spmd

    nc = bacc.Bacc("TRN2", target_bir_lowering=False, num_devices=1)
    arrays = {f"in_{name}": np.ascontiguousarray(inputs[name]) for name in _INS}
    arrays["in_shape_constants"] = shape_constants()
    io = {}
    for name, a in arrays.items():
        io[name[3:]] = nc.dram_tensor(name, a.shape, mybir.dt.from_np(a.dtype), kind="ExternalInput").ap()
    io["out"] = nc.dram_tensor("out_0", (B, T, C), F32, kind="ExternalOutput").ap()
    build_program(nc, io)
    r = run_bass_kernel_spmd(nc, [arrays], core_ids=[0])
    return r.results[0]["out_0"]
```
